# Optimizing a Trainium2 kernel written in Bass

```python
import numpy as np
import jax
import jax.numpy as jnp

def _softmax(x, axis=-1):
    return jax.nn.softmax(x, axis=axis)

def _gelu(x):
    return jax.nn.gelu(x, approximate=True)

def _silu(x):
    return jax.nn.silu(x)

def _sigmoid(x):
    return jax.nn.sigmoid(x)

def _layernorm(x, axis=-1, eps=1e-05):
    m = jnp.mean(x, axis=axis, keepdims=True)
    v = jnp.var(x, axis=axis, keepdims=True)
    return (x - m) / jnp.sqrt(v + eps)

def _scatter_add(tgt, idx, src, axis=0):
    return tgt.at[idx].add(src)

def _segment_sum(src, seg, n):
    return jax.ops.segment_sum(src, seg, n)
kernel_name = 'mk_dlrm_tower_d1_rec_r8_c7aa76'

def setup_inputs(seed: int=0):
    np.random.seed(seed)
    _w = jnp.asarray

    def _rec_inputs():
        import jax
        import jax.numpy as jnp
        _tk = jax.random.key(seed)
        dense_ctx = jax.random.normal(jax.random.fold_in(_tk, 190), (1024, 16), jnp.float32)
        ids = jnp.stack([jax.random.randint(jax.random.fold_in(_tk, 200 + f), (1024,), 0, v, jnp.int32) for f, v in enumerate([1000, 125000, 125000, 12500, 1000, 125000, 125000, 1250, 125000, 1000, 125000, 125000, 1250, 1000, 12500, 1000, 1250, 12500, 1250, 1250, 1250, 12500, 1000, 1250, 1000, 1000, 1000, 12500, 1250, 1250, 1250, 12500])], axis=1)
        tbl_0 = 0.05 * jax.random.normal(jax.random.fold_in(_tk, 500 + 0), (1000, 32), jnp.float32)
        tbl_1 = 0.05 * jax.random.normal(jax.random.fold_in(_tk, 500 + 1), (125000, 32), jnp.float32)
        tbl_2 = 0.05 * jax.random.normal(jax.random.fold_in(_tk, 500 + 2), (125000, 32), jnp.float32)
        tbl_3 = 0.05 * jax.random.normal(jax.random.fold_in(_tk, 500 + 3), (12500, 32), jnp.float32)
        tbl_4 = 0.05 * jax.random.normal(jax.random.fold_in(_tk, 500 + 4), (1000, 32), jnp.float32)
        tbl_5 = 0.05 * jax.random.normal(jax.random.fold_in(_tk, 500 + 5), (125000, 32), jnp.float32)
        tbl_6 = 0.05 * jax.random.normal(jax.random.fold_in(_tk, 500 + 6), (125000, 32), jnp.float32)
        tbl_7 = 0.05 * jax.random.normal(jax.random.fold_in(_tk, 500 + 7), (1250, 32), jnp.float32)
        tbl_8 = 0.05 * jax.random.normal(jax.random.fold_in(_tk, 500 + 8), (125000, 32), jnp.float32)
        tbl_9 = 0.05 * jax.random.normal(jax.random.fold_in(_tk, 500 + 9), (1000, 32), jnp.float32)
        tbl_10 = 0.05 * jax.random.normal(jax.random.fold_in(_tk, 500 + 10), (125000, 32), jnp.float32)
        tbl_11 = 0.05 * jax.random.normal(jax.random.fold_in(_tk, 500 + 11), (125000, 32), jnp.float32)
        tbl_12 = 0.05 * jax.random.normal(jax.random.fold_in(_tk, 500 + 12), (1250, 32), jnp.float32)
        tbl_13 = 0.05 * jax.random.normal(jax.random.fold_in(_tk, 500 + 13), (1000, 32), jnp.float32)
        tbl_14 = 0.05 * jax.random.normal(jax.random.fold_in(_tk, 500 + 14), (12500, 32), jnp.float32)
        tbl_15 = 0.05 * jax.random.normal(jax.random.fold_in(_tk, 500 + 15), (1000, 32), jnp.float32)
        tbl_16 = 0.05 * jax.random.normal(jax.random.fold_in(_tk, 500 + 16), (1250, 32), jnp.float32)
        tbl_17 = 0.05 * jax.random.normal(jax.random.fold_in(_tk, 500 + 17), (12500, 32), jnp.float32)
        tbl_18 = 0.05 * jax.random.normal(jax.random.fold_in(_tk, 500 + 18), (1250, 32), jnp.float32)
        tbl_19 = 0.05 * jax.random.normal(jax.random.fold_in(_tk, 500 + 19), (1250, 32), jnp.float32)
        tbl_20 = 0.05 * jax.random.normal(jax.random.fold_in(_tk, 500 + 20), (1250, 32), jnp.float32)
        tbl_21 = 0.05 * jax.random.normal(jax.random.fold_in(_tk, 500 + 21), (12500, 32), jnp.float32)
        tbl_22 = 0.05 * jax.random.normal(jax.random.fold_in(_tk, 500 + 22), (1000, 32), jnp.float32)
        tbl_23 = 0.05 * jax.random.normal(jax.random.fold_in(_tk, 500 + 23), (1250, 32), jnp.float32)
        tbl_24 = 0.05 * jax.random.normal(jax.random.fold_in(_tk, 500 + 24), (1000, 32), jnp.float32)
        tbl_25 = 0.05 * jax.random.normal(jax.random.fold_in(_tk, 500 + 25), (1000, 32), jnp.float32)
        tbl_26 = 0.05 * jax.random.normal(jax.random.fold_in(_tk, 500 + 26), (1000, 32), jnp.float32)
        tbl_27 = 0.05 * jax.random.normal(jax.random.fold_in(_tk, 500 + 27), (12500, 32), jnp.float32)
        tbl_28 = 0.05 * jax.random.normal(jax.random.fold_in(_tk, 500 + 28), (1250, 32), jnp.float32)
        tbl_29 = 0.05 * jax.random.normal(jax.random.fold_in(_tk, 500 + 29), (1250, 32), jnp.float32)
        tbl_30 = 0.05 * jax.random.normal(jax.random.fold_in(_tk, 500 + 30), (1250, 32), jnp.float32)
        tbl_31 = 0.05 * jax.random.normal(jax.random.fold_in(_tk, 500 + 31), (12500, 32), jnp.float32)
        _rk = jax.random.fold_in(_tk, 7)
        W_top1 = 0.0606339 * jax.random.normal(jax.random.fold_in(_tk, 801), (272, 512), jnp.float32)
        W_top2 = 0.0441942 * jax.random.normal(jax.random.fold_in(_tk, 802), (512, 256), jnp.float32)
        W_top3 = 0.0625 * jax.random.normal(jax.random.fold_in(_tk, 803), (256, 1), jnp.float32)
        b_top1 = jnp.zeros((512,), jnp.float32)
        b_top2 = jnp.zeros((256,), jnp.float32)
        return (dense_ctx, ids, tbl_0, tbl_1, tbl_2, tbl_3, tbl_4, tbl_5, tbl_6, tbl_7, tbl_8, tbl_9, tbl_10, tbl_11, tbl_12, tbl_13, tbl_14, tbl_15, tbl_16, tbl_17, tbl_18, tbl_19, tbl_20, tbl_21, tbl_22, tbl_23, tbl_24, tbl_25, tbl_26, tbl_27, tbl_28, tbl_29, tbl_30, tbl_31, W_top1, b_top1, W_top2, b_top2, W_top3)
    dense_ctx, ids, tbl_0, tbl_1, tbl_2, tbl_3, tbl_4, tbl_5, tbl_6, tbl_7, tbl_8, tbl_9, tbl_10, tbl_11, tbl_12, tbl_13, tbl_14, tbl_15, tbl_16, tbl_17, tbl_18, tbl_19, tbl_20, tbl_21, tbl_22, tbl_23, tbl_24, tbl_25, tbl_26, tbl_27, tbl_28, tbl_29, tbl_30, tbl_31, W_top1, b_top1, W_top2, b_top2, W_top3 = _rec_inputs()

    def _L0_rec_setup():
        import jax, jax.numpy as jnp
        import numpy as np
        B, F, D = (512, 32, 32)
        LAYER_SIZE = [128, 128]

        def _cin_forward(inputs, filters):
            x0 = inputs
            prev = inputs
            outs = []
            for W in filters:
                z = jnp.einsum('bhd,bmd->bhmd', x0, prev)
                b, h, m, d = z.shape
                z = z.reshape(b, h * m, d)
                cur = jnp.einsum('bpd,pn->bnd', z, W[0])
                cur = jax.nn.relu(cur)
                prev = cur
                outs.append(cur)
            result = jnp.concatenate(outs, axis=1)
            return jnp.sum(result, axis=-1)
        key = jax.random.key(seed)
        k1, k2, k3 = jax.random.split(key, 3)
        inputs = jax.random.normal(k1, (B, F, D), dtype=jnp.float32)
        field_nums = [F] + LAYER_SIZE
        filter_0 = jax.random.normal(k2, (1, field_nums[0] * field_nums[0], field_nums[1]), dtype=jnp.float32) * 0.05
        filter_1 = jax.random.normal(k3, (1, field_nums[0] * field_nums[1], field_nums[2]), dtype=jnp.float32) * 0.05
        return {'inputs': inputs, 'filter_0': filter_0, 'filter_1': filter_1}
    _L0_rec_all = _L0_rec_setup()
    _L0_rec_in = {k: v for k, v in _L0_rec_all.items() if k in ('filter_0', 'filter_1')}
    del _L0_rec_all
    return {'dense_ctx': dense_ctx, 'ids': ids, 'tbl_0': tbl_0, 'tbl_1': tbl_1, 'tbl_2': tbl_2, 'tbl_3': tbl_3, 'tbl_4': tbl_4, 'tbl_5': tbl_5, 'tbl_6': tbl_6, 'tbl_7': tbl_7, 'tbl_8': tbl_8, 'tbl_9': tbl_9, 'tbl_10': tbl_10, 'tbl_11': tbl_11, 'tbl_12': tbl_12, 'tbl_13': tbl_13, 'tbl_14': tbl_14, 'tbl_15': tbl_15, 'tbl_16': tbl_16, 'tbl_17': tbl_17, 'tbl_18': tbl_18, 'tbl_19': tbl_19, 'tbl_20': tbl_20, 'tbl_21': tbl_21, 'tbl_22': tbl_22, 'tbl_23': tbl_23, 'tbl_24': tbl_24, 'tbl_25': tbl_25, 'tbl_26': tbl_26, 'tbl_27': tbl_27, 'tbl_28': tbl_28, 'tbl_29': tbl_29, 'tbl_30': tbl_30, 'tbl_31': tbl_31, 'W_top1': W_top1, 'b_top1': b_top1, 'W_top2': W_top2, 'b_top2': b_top2, 'W_top3': W_top3, 'L0_rec_filter_0': _L0_rec_in['filter_0'], 'L0_rec_filter_1': _L0_rec_in['filter_1']}

def reference(dense_ctx, ids, tbl_0, tbl_1, tbl_2, tbl_3, tbl_4, tbl_5, tbl_6, tbl_7, tbl_8, tbl_9, tbl_10, tbl_11, tbl_12, tbl_13, tbl_14, tbl_15, tbl_16, tbl_17, tbl_18, tbl_19, tbl_20, tbl_21, tbl_22, tbl_23, tbl_24, tbl_25, tbl_26, tbl_27, tbl_28, tbl_29, tbl_30, tbl_31, W_top1, b_top1, W_top2, b_top2, W_top3, L0_rec_filter_0, L0_rec_filter_1):
    import jax
    import jax.numpy as jnp

    def _L0_rec_ref(inputs, filter_0, filter_1):
        import jax, jax.numpy as jnp
        import numpy as np
        B, F, D = (512, 32, 32)
        LAYER_SIZE = [128, 128]

        def _cin_forward(inputs, filters):
            x0 = inputs
            prev = inputs
            outs = []
            for W in filters:
                z = jnp.einsum('bhd,bmd->bhmd', x0, prev)
                b, h, m, d = z.shape
                z = z.reshape(b, h * m, d)
                cur = jnp.einsum('bpd,pn->bnd', z, W[0])
                cur = jax.nn.relu(cur)
                prev = cur
                outs.append(cur)
            result = jnp.concatenate(outs, axis=1)
            return jnp.sum(result, axis=-1)
        return _cin_forward(inputs, (filter_0, filter_1))
    e = jnp.stack([tbl_0[ids[:, 0]], tbl_1[ids[:, 1]], tbl_2[ids[:, 2]], tbl_3[ids[:, 3]], tbl_4[ids[:, 4]], tbl_5[ids[:, 5]], tbl_6[ids[:, 6]], tbl_7[ids[:, 7]], tbl_8[ids[:, 8]], tbl_9[ids[:, 9]], tbl_10[ids[:, 10]], tbl_11[ids[:, 11]], tbl_12[ids[:, 12]], tbl_13[ids[:, 13]], tbl_14[ids[:, 14]], tbl_15[ids[:, 15]], tbl_16[ids[:, 16]], tbl_17[ids[:, 17]], tbl_18[ids[:, 18]], tbl_19[ids[:, 19]], tbl_20[ids[:, 20]], tbl_21[ids[:, 21]], tbl_22[ids[:, 22]], tbl_23[ids[:, 23]], tbl_24[ids[:, 24]], tbl_25[ids[:, 25]], tbl_26[ids[:, 26]], tbl_27[ids[:, 27]], tbl_28[ids[:, 28]], tbl_29[ids[:, 29]], tbl_30[ids[:, 30]], tbl_31[ids[:, 31]]], axis=1)
    z = _L0_rec_ref(e, L0_rec_filter_0, L0_rec_filter_1)
    z = z.reshape(z.shape[0], -1)
    h = jnp.concatenate([z, dense_ctx], axis=1)
    h = jnp.maximum(h @ W_top1 + b_top1, 0.0)
    h = jnp.maximum(h @ W_top2 + b_top2, 0.0)
    y = h @ W_top3
    return y

_drawn_inputs = setup_inputs


def setup_inputs(seed=0):
    import zlib

    import numpy as np

    out = dict(_drawn_inputs(seed))
    spreads = {'b_top1': (0.0, 0.436), 'b_top2': (0.0, 0.427)}
    factors = {'tbl_0': 5.937,
     'tbl_1': 5.811,
     'tbl_2': 5.743,
     'tbl_3': 6.152,
     'tbl_4': 6.409,
     'tbl_5': 5.885,
     'tbl_6': 5.998,
     'tbl_7': 6.093,
     'tbl_8': 6.172,
     'tbl_9': 5.997,
     'tbl_10': 5.981,
     'tbl_11': 6.311,
     'tbl_12': 5.972,
     'tbl_13': 5.941,
     'tbl_14': 6.063,
     'tbl_15': 5.857,
     'tbl_16': 6.273,
     'tbl_17': 6.343,
     'tbl_18': 6.203,
     'tbl_19': 6.534,
     'tbl_20': 5.996,
     'tbl_21': 6.063,
     'tbl_22': 5.993,
     'tbl_23': 6.246,
     'tbl_24': 6.012,
     'tbl_25': 5.949,
     'tbl_26': 5.854,
     'tbl_27': 6.259,
     'tbl_28': 6.161,
     'tbl_29': 6.179,
     'tbl_30': 6.196,
     'tbl_31': 5.768,
     'L0_rec_filter_1': 8.0}
    for name, (base, spread) in spreads.items():
        noise = np.random.default_rng([zlib.crc32(name.encode()), seed]).standard_normal(out[name].shape)
        drawn = base * np.exp(spread * noise) if base else spread * noise
        out[name] = jnp.asarray(drawn.astype(out[name].dtype))
    for name, factor in factors.items():
        out[name] = (out[name] * factor).astype(out[name].dtype)
    return out
```

```python
import concourse.bass as bass
from concourse import mybir
from contextlib import ExitStack

BATCH, FIELDS, WIDTH, MAPS = 1024, 32, 32, 128
DENSE, HID1, HID2 = 16, 512, 256
P = 128
BATCH_TILES = BATCH // P
TILES = 4
GROUPS_OF_BT = WIDTH // TILES
GROUPS = BATCH_TILES * GROUPS_OF_BT
COLS = TILES * P
DIST = P // FIELDS
BLOCKS = 5
WRAP = 52
PAIR = 2
UNIT_H = COLS // MAPS
FILLS = FIELDS // UNIT_H
SLOTS = TILES * FILLS
RING = 4
DVE_UNITS = FIELDS // 2
TURN_AT = 7
REPEAT_AT = 11
SHIFT_AT = [11, 13, 15, 18, 20]
CONTRACT_AT = [16, 18, 20, 22, 24]
FIELDS_AFTER, LOW_AFTER, PARTS_AFTER, REPEATED_AFTER = 1, 4, 7, 9
PAIRS_AFTER = [12, 14, 16, 18, 20]
MAPS_AFTER, SPLIT_AFTER = 25, 26
VOCAB = [1000, 125000, 125000, 12500, 1000, 125000, 125000, 1250, 125000, 1000, 125000, 125000,
         1250, 1000, 12500, 1000, 1250, 12500, 1250, 1250, 1250, 12500, 1000, 1250, 1000, 1000,
         1000, 12500, 1250, 1250, 1250, 12500]


def positive(count):
    return not isinstance(count, int) or count > 0


def dlrm_tower(nc, dense, ids, tables, w_top1, b_top1, w_top2, b_top2, w_top3, filter0, filter1, out):
    fp32, fp32r, int32 = mybir.dt.float32, mybir.dt.float32r, mybir.dt.int32
    ALU, ACT, AX = mybir.AluOpType, mybir.ActivationFunctionType, mybir.AxisListType

    with ExitStack() as ctx:
        def sb(name, shape, dt=fp32):
            return ctx.enter_context(nc.sbuf_tensor(name, shape, dt))

        def pb(name, dt=fp32):
            return ctx.enter_context(nc.psum_tensor(name, [P, COLS], dt))

        def sem(name):
            return ctx.enter_context(nc.semaphore(name))

        identity = sb("identity", [P, P])
        field_match = sb("field_match", [P, FIELDS])
        match_wrapped = sb("match_wrapped", [P, PAIR, WRAP])
        spread = sb("spread", [P, PAIR, 1 + BLOCKS, P], fp32r)
        pair_upper = sb("pair_upper", [P, BLOCKS, MAPS])
        pair_lower = sb("pair_lower", [P, BLOCKS, MAPS])
        pair_filter = sb("pair_filter", [P, BLOCKS, MAPS])
        filter1_full = sb("filter1_full", [P, FIELDS * MAPS])
        filter1_high = sb("filter1_high", [P, FIELDS * MAPS], fp32r)
        filter1_low = sb("filter1_low", [P, FIELDS * MAPS], fp32r)
        top1 = sb("top1", [P, 3, HID1])
        top2 = sb("top2", [P, HID1 // P, HID2])
        top3 = sb("top3", [P, HID2 // P])
        bias1 = sb("bias1", [P, HID1 // P])
        bias2 = sb("bias2", [P, HID2 // P])
        ids_all = sb("ids_all", [P, BATCH_TILES, FIELDS], int32)
        ids_now = sb("ids_now", [P, FIELDS], int32)
        gathered = sb("gathered", [P, FIELDS, WIDTH])
        embedded = sb("embedded", [P, FIELDS, BATCH_TILES * WIDTH])
        fields = sb("fields", [P, 2, TILES, FIELDS])
        parts = sb("parts", [P, PAIR, PAIR, 2, FIELDS], fp32r)
        parts_t = sb("parts_t", [P, PAIR * P], fp32r)
        repeated = sb("repeated", [P, COLS])
        pairs = sb("pairs", [P, 2, COLS])
        maps_high = sb("maps_high", [P, 2, COLS], fp32r)
        maps_low = sb("maps_low", [P, 2, COLS], fp32r)
        pooled0 = sb("pooled0", [P, BATCH])
        lanes = sb("lanes", [P, 2, 2, MAPS])
        lanes_sum = sb("lanes_sum", [P, 2, MAPS])
        scaled = sb("scaled", [P, 2, FILLS // 2 * COLS])
        fold1 = sb("fold1", [P, 1024])
        fold2 = sb("fold2", [P, 512])
        fold3 = sb("fold3", [P, 256])
        fold4 = sb("fold4", [P, 2, MAPS])
        total = sb("total", [P, MAPS])
        pooled1 = sb("pooled1", [P, BATCH])
        dense_in = sb("dense_in", [P, BATCH_TILES, P])
        dense_t = sb("dense_t", [P, BATCH])
        pooled1_t = sb("pooled1_t", [P, BATCH])
        hidden1 = sb("hidden1", [P, HID1 // P, BATCH])
        hidden2 = sb("hidden2", [P, HID2 // P, BATCH])
        y_row = sb("y_row", [1, BATCH])

        inner = [pb(f"inner{i}") for i in range(RING)]
        turned = [pb(f"turned{i}") for i in range(3)]
        maps_sum = pb("maps_sum")

        ids_loaded = sem("ids_loaded")
        filter0_loaded = sem("filter0_loaded")
        filter1_loaded = sem("filter1_loaded")
        top_loaded = sem("top_loaded")
        rows_gathered = sem("rows_gathered")
        embedded_ready = sem("embedded_ready")
        stored = sem("stored")
        identity_blank = sem("identity_blank")
        identity_ready = sem("identity_ready")
        match_blank = sem("match_blank")
        blanks_ready = sem("blanks_ready")
        pair_filter_ready = sem("pair_filter_ready")
        high_ready = sem("high_ready")
        low_ready = sem("low_ready")
        ids_ready = sem("ids_ready")
        match_ready = sem("match_ready")
        spread_ready = sem("spread_ready")
        fields_ready = sem("fields_ready")
        low_parts_ready = sem("low_parts_ready")
        parts_turned = sem("parts_turned")
        parts_ready = sem("parts_ready")
        turned_ready = sem("turned_ready")
        repeated_ready = sem("repeated_ready")
        pairs_ready = sem("pairs_ready")
        block_contracted = sem("block_contracted")
        maps_high_ready = sem("maps_high_ready")
        maps_low_ready = sem("maps_low_ready")
        pooled0_added = sem("pooled0_added")
        inner_ready = sem("inner_ready")
        unit_added = sem("unit_added")
        bank_scaled = sem("bank_scaled")
        folded = sem("folded")
        lanes_summed = sem("lanes_summed")
        total_ready = sem("total_ready")
        pooled1_added = sem("pooled1_added")
        top_turned = sem("top_turned")
        top_turned_copied = sem("top_turned_copied")
        hidden1_summed = sem("hidden1_summed")
        hidden1_ready = sem("hidden1_ready")
        hidden2_summed = sem("hidden2_summed")
        hidden2_ready = sem("hidden2_ready")
        y_summed = sem("y_summed")
        y_ready = sem("y_ready")

        def distances(which, first, step):
            a = match_wrapped[:, which, first:first + FIELDS]
            return bass.AP(tensor=a.tensor, offset=a.offset, ap=[a.ap[0], [step, DIST], [1, FIELDS]])

        def parts_by_tile(part):
            return parts[:, :, :, part, :].rearrange("p m q f -> p q m f")

        def pair_rows():
            for s in range(FIELDS // 2 + 1):
                straight = FIELDS - s if s < FIELDS // 2 else FIELDS // 2
                at = (s % DIST) * FIELDS
                yield s, at, straight, s, FIELDS * s
                if 0 < s < FIELDS // 2:
                    i = FIELDS - s
                    yield s, at + i, s, 33 * i + s - FIELDS, 33 * i + FIELDS * (s - FIELDS)

        pair_loads = list(pair_rows())

        def load_pairs(queue, dst, lower, picked):
            for s, at, count, upper_row, lower_row in picked:
                if lower and s == 0:
                    continue
                row = lower_row if lower else upper_row
                src = bass.AP(tensor=filter0.tensor, offset=row * MAPS,
                              ap=[[33 * MAPS, count], [1, MAPS]])
                queue.dma_start(dst[at:at + count, s // DIST, :], src).then_inc(filter0_loaded, 16)

        PAIR_LOADS = 2 * len(pair_loads) - 1

        block = ctx.enter_context(nc.Block())

        @block.sync
        def _(sp):
            sp.dma_start(ids_all[:, :, :], ids.rearrange("(t p) f -> p t f", p=P)).then_inc(ids_loaded, 16)
            sp.wait_ge(blanks_ready, 3)
            load_pairs(sp, pair_upper, False, pair_loads)
            sp.dma_start(filter1_full[:, :].rearrange("m (h n) -> m h n", h=FIELDS),
                         filter1.rearrange("o (h m) n -> m (o h) n", m=MAPS)).then_inc(filter1_loaded, 16)
            sp.wait_ge(blanks_ready, 5)
            for k in range(2):
                sp.dma_start(top1[:, k, :], w_top1[k * P:(k + 1) * P, :]).then_inc(top_loaded, 16)
            sp.dma_start(top1[0:DENSE, 2, :], w_top1[2 * P:2 * P + DENSE, :]).then_inc(top_loaded, 16)
            sp.dma_start(top2[:, :, :], w_top2.rearrange("(k p) n -> p k n", p=P)).then_inc(top_loaded, 16)
            sp.dma_start(top3[:, :], w_top3.rearrange("(k p) n -> p (k n)", p=P),
                         allow_slow_non_contiguous=True).then_inc(top_loaded, 16)
            sp.dma_start(bias1[:, :], b_top1.rearrange("(k p) -> p k", p=P),
                         allow_slow_non_contiguous=True).then_inc(top_loaded, 16)
            sp.dma_start(bias2[:, :], b_top2.rearrange("(k p) -> p k", p=P),
                         allow_slow_non_contiguous=True).then_inc(top_loaded, 16)
            sp.dma_start(dense_in[:, :, 0:DENSE],
                         dense.rearrange("(t p) f -> p t f", p=P)).then_inc(top_loaded, 16)
            with sp.Fori(0, BATCH_TILES) as bt:
                sp.wait_ge(rows_gathered, (bt + 1) * (16 * FIELDS))
                sp.dma_start(embedded[:, :, bass.ds(bt * WIDTH, WIDTH)],
                             gathered[:, :, :]).then_inc(embedded_ready, 16)
            sp.wait_ge(y_ready, 2)
            sp.dma_start(out.rearrange("b o -> o b"), y_row[0:1, :]).then_inc(stored, 16)
            sp.wait_ge(stored, 16)

        @block.gpsimd
        def _(pool):
            nc.gpsimd.memset(identity[:, :], 1.0).then_inc(identity_blank, 1)
            pool.wait_ge(identity_blank, 1)
            nc.gpsimd.affine_select(out=identity[:, :], in_=identity[:, :], compare_op=ALU.is_equal,
                                    fill=0.0, base=0, pattern=[[-1, P]],
                                    channel_multiplier=1).then_inc(identity_ready, 1)

            def next_ids(bt):
                pool.wait_ge(ids_ready, bt) if positive(bt) else None
                nc.gpsimd.tensor_copy(ids_now[:, :], ids_all[:, bass.ds(bt, 1), :].rearrange(
                    "p t f -> p (t f)")).then_inc(ids_ready, 1)
                pool.wait_ge(ids_ready, bt + 1)

            def gather(f):
                pool.indirect_dma_start(gathered[:, f, :], None, tables[f][:, :],
                                        bass.IndirectOffsetOnAxis(ap=ids_now[:, f:f + 1], axis=0)
                                        ).then_inc(rows_gathered, 16)

            def fold_tile(tile, par):
                pool.wait_ge(bank_scaled, (tile + 1) * (FILLS // 2))
                if positive(tile):
                    pool.wait_ge(folded, tile * 4)
                nc.gpsimd.tensor_tensor(fold1[:, :], scaled[:, par, 0:1024], scaled[:, par, 1024:2048],
                                        ALU.add).then_inc(folded, 1)
                pool.wait_ge(folded, tile * 4 + 1)
                nc.gpsimd.tensor_tensor(fold2[:, :], fold1[:, 0:512], fold1[:, 512:1024],
                                        ALU.add).then_inc(folded, 1)
                pool.wait_ge(folded, tile * 4 + 2)
                nc.gpsimd.tensor_tensor(fold3[:, :], fold2[:, 0:256], fold2[:, 256:512],
                                        ALU.add).then_inc(folded, 1)
                pool.wait_ge(folded, tile * 4 + 3)
                if positive(tile - 1):
                    pool.wait_ge(total_ready, tile - 1)
                nc.gpsimd.tensor_tensor(fold4[:, par, :], fold3[:, 0:MAPS], fold3[:, MAPS:2 * MAPS],
                                        ALU.add).then_inc(folded, 1)

            def batch_tile(bt, more):
                if more:
                    pool.wait_ge(embedded_ready, (bt + 1) * 16)
                    next_ids(bt + 1)
                for g in range(GROUPS_OF_BT):
                    for j in range(TILES):
                        fold_tile(bt * (GROUPS_OF_BT * TILES) + g * TILES + j, j % 2)
                        n = g * TILES + j
                        for f in range(5 * n // 4, 5 * (n + 1) // 4):
                            if more and f < FIELDS:
                                gather(f)

            pool.wait_ge(ids_loaded, 16)
            next_ids(0)
            for f in range(FIELDS):
                gather(f)
            batch_tile(0, True)
            with pool.Fori(1, BATCH_TILES - 1) as bt:
                batch_tile(bt, True)
            batch_tile(BATCH_TILES - 1, False)

        @block.scalar
        def _(act):
            act.wait_ge(blanks_ready, 3)
            load_pairs(act, pair_lower, True, pair_loads)
            act.wait_ge(match_ready, 4)
            for which in range(PAIR):
                nc.scalar.activation(spread[:, which, 0, :].rearrange("p (s f) -> p s f", s=DIST),
                                     distances(which, 0, 0), ACT.Copy)
                for t in range(BLOCKS):
                    last = nc.scalar.activation(spread[:, which, 1 + t, :].rearrange("p (s f) -> p s f", s=DIST),
                                                distances(which, DIST * t, 1), ACT.Copy)
            last.then_inc(spread_ready, 1)
            act.wait_ge(filter1_loaded, 16)
            nc.scalar.activation(filter1_high[:, :], filter1_full[:, :], ACT.Copy).then_inc(high_ready, 1)

            def take_fields(G, par):
                act.wait_ge(embedded_ready, (G // GROUPS_OF_BT + 1) * 16)
                if positive(G - 1):
                    act.wait_ge(unit_added, (G - 1) * (TILES * DVE_UNITS))
                    act.wait_ge(bank_scaled, (G - 1) * (SLOTS // 2))
                src = embedded[:, :, bass.ds(G * TILES, TILES)].rearrange("p f j -> p j f")
                if positive(G):
                    act.wait_ge(parts_turned, G)
                act.wait_ge(embedded_ready, 16)
                nc.scalar.activation(fields[:, par, :, :], src, ACT.Copy)
                src = src.rearrange("p (q m) f -> p q m f", m=PAIR)
                nc.scalar.activation(parts_by_tile(0), src, ACT.Copy).then_inc(fields_ready, 1)

            def take_parts(G):
                act.wait_ge(parts_turned, G + 1)
                if positive(G):
                    act.wait_ge(turned_ready, G * (BLOCKS + 1))
                nc.scalar.activation(parts_t[:, :], turned[0][:, 0:PAIR * P],
                                     ACT.Copy).then_inc(parts_ready, 1)

            def take_repeated(G):
                act.wait_ge(turned_ready, G * (BLOCKS + 1) + 1)
                if positive(G):
                    act.wait_ge(pairs_ready, G * BLOCKS)
                nc.scalar.activation(repeated[:, :], turned[1][:, :], ACT.Copy).then_inc(repeated_ready, 1)

            def take_maps(G, par):
                act.wait_ge(block_contracted, (G + 1) * BLOCKS)
                if positive(G - 1):
                    act.wait_ge(inner_ready, (G - 1) * SLOTS)
                nc.scalar.activation(maps_high[:, par, :], maps_sum[:, :],
                                     ACT.Relu).then_inc(maps_high_ready, 1)

            def group(G, par, more):
                for k in range(1, SLOTS, 2):
                    j, b = k // FILLS, k % FILLS
                    tile = G * TILES + j
                    if b == 1 and positive(tile - 1):
                        act.wait_ge(folded, (tile - 2) * 4 + 1)
                    act.wait_ge(inner_ready, G * SLOTS + (k + 1))
                    for c in range(UNIT_H):
                        h = b * UNIT_H + c
                        at = b // 2 * COLS + c * MAPS
                        last = nc.scalar.activation(scaled[:, j % 2, at:at + MAPS],
                                                    inner[k % RING][:, c * MAPS:(c + 1) * MAPS],
                                                    ACT.Copy, scale=fields[:, par, j, h:h + 1])
                    last.then_inc(bank_scaled, 1)
                    if more and k == FIELDS_AFTER:
                        take_fields(G + 1, 1 - par)
                    if more and k == PARTS_AFTER:
                        take_parts(G + 1)
                    if more and k == REPEATED_AFTER:
                        take_repeated(G + 1)
                    if more and k == MAPS_AFTER:
                        take_maps(G + 1, 1 - par)

            take_fields(0, 0)
            take_parts(0)
            take_repeated(0)
            take_maps(0, 0)
            group(0, 0, True)
            group(1, 1, True)
            with act.Fori(1, GROUPS // 2 - 1) as pair:
                group(pair * 2, 0, True)
                group(pair * 2 + 1, 1, True)
            group(GROUPS - 2, 0, True)
            group(GROUPS - 1, 1, False)

            act.wait_ge(top_loaded, 16 * 8)
            for n in range(HID1 // P * 2):
                act.wait_ge(hidden1_summed, n + 1)
                half, o = n // (HID1 // P), n % (HID1 // P)
                nc.scalar.activation(hidden1[:, o, half * 512:(half + 1) * 512], inner[n % RING][:, :],
                                     ACT.Relu, bias=bias1[:, o:o + 1]).then_inc(hidden1_ready, 1)
            for n in range(HID2 // P * 2):
                act.wait_ge(hidden2_summed, n + 1)
                half, o = n // (HID2 // P), n % (HID2 // P)
                nc.scalar.activation(hidden2[:, o, half * 512:(half + 1) * 512], inner[n % RING][:, :],
                                     ACT.Relu, bias=bias2[:, o:o + 1]).then_inc(hidden2_ready, 1)
            for half in range(2):
                act.wait_ge(y_summed, half + 1)
                nc.scalar.activation(y_row[0:1, half * 512:(half + 1) * 512], turned[half][0:1, :],
                                     ACT.Copy).then_inc(y_ready, 1)

        @block.vector
        def _(dve):
            nc.vector.memset(pair_upper[:, BLOCKS - 1, :], 0.0).then_inc(blanks_ready, 1)
            nc.vector.memset(pair_lower[:, BLOCKS - 1, :], 0.0).then_inc(blanks_ready, 1)
            nc.vector.memset(pair_lower[:, 0, :], 0.0).then_inc(blanks_ready, 1)
            nc.vector.memset(dense_in[:, :, :], 0.0).then_inc(blanks_ready, 1)
            nc.vector.memset(top1[:, 2, :], 0.0).then_inc(blanks_ready, 1)
            nc.vector.memset(pooled0[:, :], 0.0).then_inc(pooled0_added, 1)
            nc.vector.memset(pooled1[:, :], 0.0).then_inc(pooled1_added, 1)
            nc.vector.memset(match_wrapped[:, :, :], 0.0).then_inc(match_blank, 1)
            dve.wait_ge(identity_ready, 1)
            nc.vector.tensor_reduce(field_match[:, :], identity[:, :].rearrange("p (q f) -> p f q", f=FIELDS),
                                    AX.X, ALU.add).then_inc(match_blank, 1)
            dve.wait_ge(match_blank, 2)
            for which in range(PAIR):
                rows = slice(which * P // 2, (which + 1) * P // 2)
                nc.vector.tensor_copy(match_wrapped[rows, which, 0:FIELDS],
                                      field_match[rows, :]).then_inc(match_ready, 1)
                nc.vector.tensor_copy(match_wrapped[rows, which, FIELDS:WRAP],
                                      field_match[rows, 0:WRAP - FIELDS]).then_inc(match_ready, 1)
            dve.wait_ge(filter0_loaded, 16 * PAIR_LOADS)
            nc.vector.tensor_tensor(pair_filter[:, :, :], pair_upper[:, :, :], pair_lower[:, :, :],
                                    ALU.add).then_inc(pair_filter_ready, 1)
            dve.wait_ge(high_ready, 1)
            nc.vector.tensor_tensor(filter1_low[:, :], filter1_full[:, :],
                                    filter1_high[:, :].bitcast(fp32), ALU.subtract).then_inc(low_ready, 1)

            def low_parts(G, par):
                dve.wait_ge(fields_ready, G + 1)
                full = fields[:, par, :, :].rearrange("p (q m) f -> p q m f", m=PAIR)
                nc.vector.tensor_tensor(parts_by_tile(1), full, parts_by_tile(0).bitcast(fp32),
                                        ALU.subtract).then_inc(low_parts_ready, 1)

            def make_pairs(G, t):
                dve.wait_ge(turned_ready, G * (BLOCKS + 1) + (t + 2))
                if t == 0:
                    dve.wait_ge(repeated_ready, G + 1)
                used = max(t - 1, 0)
                if positive(G * BLOCKS + used):
                    dve.wait_ge(block_contracted, G * BLOCKS + used)
                nc.vector.tensor_tensor(pairs[:, t % 2, :], turned[(t + 2) % 3][:, :], repeated[:, :],
                                        ALU.mult).then_inc(pairs_ready, 1)

            def split_maps(G, par):
                dve.wait_ge(maps_high_ready, G + 1)
                nc.vector.scalar_tensor_tensor(out=maps_low[:, par, :], in0=maps_sum[:, :], scalar=0.0,
                                               in1=maps_high[:, par, :].bitcast(fp32), op0=ALU.max,
                                               op1=ALU.subtract).then_inc(maps_low_ready, 1)

            def pool_maps(G, j):
                dve.wait_ge(pooled0_added, G * TILES + (j + 1))
                acc = pooled0[:, bass.ds(G // GROUPS_OF_BT * P, P)]
                nc.vector.scalar_tensor_tensor(out=acc, in0=maps_sum[:, j * P:(j + 1) * P], scalar=0.0,
                                               in1=acc, op0=ALU.max, op1=ALU.add).then_inc(pooled0_added, 1)

            def sum_lanes(tile, par):
                dve.wait_ge(unit_added, (tile + 1) * DVE_UNITS)
                nc.vector.tensor_tensor(lanes_sum[:, par, :], lanes[:, par, 0, :], lanes[:, par, 1, :],
                                        ALU.add).then_inc(lanes_summed, 1)

            def sum_total(tile, par):
                dve.wait_ge(lanes_summed, tile + 1)
                dve.wait_ge(folded, (tile + 1) * 4)
                if positive(tile):
                    dve.wait_ge(pooled1_added, tile + 1)
                nc.vector.tensor_tensor(total[:, :], lanes_sum[:, par, :], fold4[:, par, :],
                                        ALU.add).then_inc(total_ready, 1)

            def pool_total(tile):
                dve.wait_ge(total_ready, tile + 1)
                dve.wait_ge(pooled1_added, tile + 1)
                acc = pooled1[:, bass.ds(tile // (GROUPS_OF_BT * TILES) * P, P)]
                nc.vector.scalar_tensor_tensor(out=acc, in0=total[:, :], scalar=0.0, in1=acc,
                                               op0=ALU.max, op1=ALU.add).then_inc(pooled1_added, 1)

            def group(G, par, more):
                for k in range(0, SLOTS, 2):
                    j, b = k // FILLS, k % FILLS
                    tile = G * TILES + j
                    dve.wait_ge(inner_ready, G * SLOTS + (k + 1))
                    if b == 0 and positive(tile - 1):
                        dve.wait_ge(lanes_summed, tile - 1)
                    for c in range(UNIT_H):
                        u = b // 2 * UNIT_H + c
                        y = inner[k % RING][:, c * MAPS:(c + 1) * MAPS]
                        x = fields[:, par, j, b * UNIT_H + c:b * UNIT_H + c + 1]
                        acc = lanes[:, j % 2, c % 2, :]
                        if u < 2:
                            nc.vector.tensor_scalar(acc, y, x, None, ALU.mult).then_inc(unit_added, 1)
                        else:
                            dve.wait_ge(unit_added, tile * DVE_UNITS + (u - 1))
                            nc.vector.scalar_tensor_tensor(out=acc, in0=y, scalar=x, in1=acc, op0=ALU.mult,
                                                           op1=ALU.add).then_inc(unit_added, 1)
                    if k < FILLS:
                        pool_maps(G, k // 2)
                    if b == 2 and positive(tile):
                        sum_lanes(tile - 1, (j - 1) % 2)
                    if b == 4 and positive(tile - 1):
                        sum_total(tile - 2, j % 2)
                    if b == 6 and positive(tile - 1):
                        pool_total(tile - 2)
                    if more and k == LOW_AFTER:
                        low_parts(G + 1, 1 - par)
                    if more and k in PAIRS_AFTER:
                        make_pairs(G + 1, PAIRS_AFTER.index(k))
                    if more and k == SPLIT_AFTER:
                        split_maps(G + 1, 1 - par)

            low_parts(0, 0)
            for t in range(BLOCKS):
                make_pairs(0, t)
            split_maps(0, 0)
            group(0, 0, True)
            group(1, 1, True)
            with dve.Fori(1, GROUPS // 2 - 1) as pair:
                group(pair * 2, 0, True)
                group(pair * 2 + 1, 1, True)
            group(GROUPS - 2, 0, True)
            group(GROUPS - 1, 1, False)
            last_tile = GROUPS * TILES - 1
            sum_lanes(last_tile, last_tile % 2)
            for tile in (last_tile - 1, last_tile):
                sum_total(tile, tile % 2)
                pool_total(tile)
            for half in range(2):
                for src, dst in ((0, pooled1_t), (1, dense_t)):
                    dve.wait_ge(top_turned, half * 2 + src + 1)
                    nc.vector.tensor_copy(dst[:, half * 512:(half + 1) * 512],
                                          turned[src][:, :]).then_inc(top_turned_copied, 1)

        @block.tensor
        def _(pe):
            def turn_parts(G):
                pe.wait_ge(fields_ready, G + 1)
                pe.wait_ge(low_parts_ready, G + 1)
                if positive(G):
                    pe.wait_ge(pairs_ready, G * BLOCKS)
                for m in range(PAIR):
                    last = nc.tensor.transpose(turned[0][:, m * P:(m + 1) * P],
                                               parts[:, m, :, :, :].rearrange("p q a f -> p (q a f)").bitcast(fp32),
                                               identity[:, :])
                last.then_inc(parts_turned, 1)

            def spread_fields(G, t):
                if t == -1:
                    pe.wait_ge(parts_ready, G + 1)
                if t == 2:
                    pe.wait_ge(repeated_ready, G + 1)
                if t > 2:
                    pe.wait_ge(pairs_ready, G * BLOCKS + (t - 2))
                for which in range(PAIR):
                    half = slice(which * PAIR * P, (which + 1) * PAIR * P)
                    last = nc.tensor.matmul(turned[(t + 2) % 3][:, half], spread[:, which, 1 + t, :],
                                            parts_t[:, :], start=True, stop=True)
                last.then_inc(turned_ready, 1)

            def contract(G, t):
                pe.wait_ge(pairs_ready, G * BLOCKS + (t + 1))
                if t == 0 and positive(G):
                    pe.wait_ge(maps_low_ready, G)
                    pe.wait_ge(pooled0_added, G * TILES + 1)
                nc.tensor.matmul(maps_sum[:, :], pair_filter[:, t, :], pairs[:, t % 2, :], start=(t == 0),
                                 stop=(t == BLOCKS - 1)).then_inc(block_contracted, 1)

            def group(G, par, more):
                pe.wait_ge(maps_low_ready, G + 1)
                for k in range(SLOTS):
                    j, b = k // FILLS, k % FILLS
                    if more and k in CONTRACT_AT:
                        contract(G + 1, CONTRACT_AT.index(k))
                    if more and k == TURN_AT:
                        turn_parts(G + 1)
                    if more and k == REPEAT_AT:
                        spread_fields(G + 1, -1)
                    if more and k in SHIFT_AT:
                        spread_fields(G + 1, SHIFT_AT.index(k))
                    if k % 2 == 0 and positive(G * SLOTS + (k - 3)):
                        pe.wait_ge(unit_added, G * (TILES * DVE_UNITS) + (k - 2) // 2 * UNIT_H)
                    if k % 2 == 1 and positive(G * SLOTS + (k - 3)):
                        pe.wait_ge(bank_scaled, G * (SLOTS // 2) + (k - 3) // 2)
                    high = maps_high[:, par, j * P:(j + 1) * P]
                    low = maps_low[:, par, j * P:(j + 1) * P]
                    cols = slice(b * COLS, (b + 1) * COLS)
                    y = inner[k % RING]
                    nc.tensor.matmul(y[:, :], low, filter1_high[:, cols], start=True, stop=False)
                    nc.tensor.matmul(y[:, :], high, filter1_low[:, cols], start=False, stop=False)
                    nc.tensor.matmul(y[:, :], high, filter1_high[:, cols], start=False,
                                     stop=True).then_inc(inner_ready, 1)

            pe.wait_ge(identity_ready, 1)
            pe.wait_ge(spread_ready, 1)
            turn_parts(0)
            spread_fields(0, -1)
            spread_fields(0, 0)
            pe.wait_ge(pair_filter_ready, 1)
            for t in range(BLOCKS):
                if t + 1 < BLOCKS:
                    spread_fields(0, t + 1)
                contract(0, t)
            pe.wait_ge(high_ready, 1)
            pe.wait_ge(low_ready, 1)
            group(0, 0, True)
            group(1, 1, True)
            with pe.Fori(1, GROUPS // 2 - 1) as pair:
                group(pair * 2, 0, True)
                group(pair * 2 + 1, 1, True)
            group(GROUPS - 2, 0, True)
            group(GROUPS - 1, 1, False)

            pe.wait_ge(top_loaded, 16 * 8)
            pe.wait_ge(pooled1_added, GROUPS * TILES + 1)
            for half in range(2):
                for src, of in ((0, pooled1), (1, dense_in)):
                    if half:
                        pe.wait_ge(top_turned_copied, src + 1)
                    for j in range(TILES):
                        bt = half * TILES + j
                        a = of[:, bt * P:(bt + 1) * P] if src == 0 else of[:, bt, :]
                        last = nc.tensor.transpose(turned[src][:, j * P:(j + 1) * P], a, identity[:, :])
                    last.then_inc(top_turned, 1)
            for half in range(2):
                pe.wait_ge(top_turned_copied, 2 * (half + 1))
                for o in range(HID1 // P):
                    n = half * (HID1 // P) + o
                    if n >= RING:
                        pe.wait_ge(hidden1_ready, n - RING + 1)
                    for k, rhs in enumerate((pooled0, pooled1_t, dense_t)):
                        last = nc.tensor.matmul(inner[n % RING][:, :], top1[:, k, o * P:(o + 1) * P],
                                                rhs[:, half * 512:(half + 1) * 512], start=(k == 0), stop=(k == 2))
                    last.then_inc(hidden1_summed, 1)
            for half in range(2):
                for o in range(HID2 // P):
                    n = half * (HID2 // P) + o
                    pe.wait_ge(hidden1_ready, HID1 // P * 2)
                    for k in range(HID1 // P):
                        last = nc.tensor.matmul(inner[n % RING][:, :], top2[:, k, o * P:(o + 1) * P],
                                                hidden1[:, k, half * 512:(half + 1) * 512],
                                                start=(k == 0), stop=(k == HID1 // P - 1))
                    last.then_inc(hidden2_summed, 1)
            for half in range(2):
                pe.wait_ge(hidden2_ready, (half + 1) * (HID2 // P))
                for k in range(HID2 // P):
                    last = nc.tensor.matmul(turned[half][0:1, :], top3[:, k:k + 1],
                                            hidden2[:, k, half * 512:(half + 1) * 512],
                                            start=(k == 0), stop=(k == HID2 // P - 1))
                last.then_inc(y_summed, 1)


_INS = (["dense_ctx", "ids"] + [f"tbl_{f}" for f in range(FIELDS)]
        + ["W_top1", "b_top1", "W_top2", "b_top2", "W_top3", "L0_rec_filter_0", "L0_rec_filter_1"])


def kernel(**inputs):
    import numpy as _np
    import concourse.bacc as _bacc
    from concourse import mybir as _mybir
    from concourse.bass_utils import run_bass_kernel_spmd as _run

    nc = _bacc.Bacc("TRN2", target_bir_lowering=False, num_devices=1)
    arrays, ap = {}, {}
    for name in _INS:
        a = _np.ascontiguousarray(inputs[name])
        arrays[f"in_{name}"] = a
        ap[name] = nc.dram_tensor(f"in_{name}", a.shape, _mybir.dt.from_np(a.dtype), kind="ExternalInput").ap()
    out = nc.dram_tensor("out_y", (BATCH, 1), _mybir.dt.float32, kind="ExternalOutput").ap()
    dlrm_tower(nc, ap["dense_ctx"], ap["ids"], [ap[f"tbl_{f}"] for f in range(FIELDS)], ap["W_top1"],
               ap["b_top1"], ap["W_top2"], ap["b_top2"], ap["W_top3"], ap["L0_rec_filter_0"],
               ap["L0_rec_filter_1"], out)
    r = _run(nc, [arrays], core_ids=[0])
    return r.results[0]["out_y"]
```

```python
import concourse.bass as bass
from concourse import mybir
from contextlib import ExitStack

BATCH, FIELDS, WIDTH, MAPS = 1024, 32, 32, 128
DENSE, HID1, HID2 = 16, 512, 256
P = 128
BATCH_TILES = BATCH // P
TILES = 4
GROUPS_OF_BT = WIDTH // TILES
GROUPS = BATCH_TILES * GROUPS_OF_BT
COLS = TILES * P
DIST = P // FIELDS
BLOCKS = 5
FULL = BLOCKS - 1
SPLIT = (0, 2)
KEPT = (1, 3)
UNIT_H = COLS // MAPS
FILLS = FIELDS // UNIT_H
SLOTS = TILES * FILLS
FIRST_EARLY = 24
EARLY_FIELDS = GROUPS_OF_BT * TILES - FIRST_EARLY + 1
V_RING, S_RING = 2, 4
RING = V_RING + S_RING
OWNER = "XSVSSVSV"
DVE_UNITS = OWNER.count("V") * UNIT_H
ACT_BANKS = FILLS - OWNER.count("V")
FOLD_BANKS = OWNER.count("S")
CONTRACT_AT = [8, 12, 19, 22, 25]
TURN_AT = 16
BLOCK_HIGH_AFTER = [30, 12]
FIELDS_AFTER, LAST_HIGH_AFTER, MAPS_AFTER = 6, 20, 25
EARLY_AFTER, TURNED_AFTER = 11, 17
PAIRS_AFTER = [29, 5, 10, 15, 18]
BLOCK_LOW_AFTER = [31, 13]
LAST_LOW_AFTER, SPLIT_AFTER, POOL_MAPS_AFTER = 21, 26, 2
LANES_AFTER, LANES_SUM_AFTER, TOTAL_AFTER, POOL_TOTAL_AFTER = 7, 13, 23, 23


def slots_of(owners, end):
    return sum(OWNER[k % FILLS] in owners for k in range(end))


def bank_of(k):
    if OWNER[k % FILLS] == "V":
        return slots_of("V", k) % V_RING
    return V_RING + slots_of("SX", k) % S_RING


def split_used(G, t):
    n = SPLIT.index(t)
    return G * BLOCKS + (SPLIT[n - 1] + 1 if n else SPLIT[-1] + 1 - BLOCKS)


def positive(count):
    return not isinstance(count, int) or count > 0


def dlrm_tower(nc, dense, ids, tables, w_top1, b_top1, w_top2, b_top2, w_top3, filter0, filter1, out):
    fp32, fp32r, int32 = mybir.dt.float32, mybir.dt.float32r, mybir.dt.int32
    ALU, ACT, AX = mybir.AluOpType, mybir.ActivationFunctionType, mybir.AxisListType

    with ExitStack() as ctx:
        def sb(name, shape, dt=fp32):
            return ctx.enter_context(nc.sbuf_tensor(name, shape, dt))

        def pb(name, dt=fp32):
            return ctx.enter_context(nc.psum_tensor(name, [P, COLS], dt))

        def sem(name):
            return ctx.enter_context(nc.semaphore(name))

        identity = sb("identity", [P, P])
        field_match = sb("field_match", [P, FIELDS])
        pair_filter = sb("pair_filter", [P, len(KEPT), MAPS])
        split_high = sb("split_high", [P, len(SPLIT), MAPS], fp32r)
        split_low = sb("split_low", [P, len(SPLIT), MAPS], fp32r)
        last_high = sb("last_high", [P, MAPS], fp32r)
        last_filter = sb("last_filter", [P, MAPS], fp32r)
        takes_high = sb("takes_high", [P, 1])
        takes_low = sb("takes_low", [P, 1])
        filter1_full = sb("filter1_full", [P, FIELDS * MAPS])
        filter1_high = sb("filter1_high", [P, FIELDS * MAPS], fp32r)
        filter1_low = sb("filter1_low", [P, FIELDS * MAPS], fp32r)
        top1 = sb("top1", [P, 3, HID1])
        top2 = sb("top2", [P, HID1 // P, HID2])
        top3 = sb("top3", [P, HID2 // P])
        bias1 = sb("bias1", [P, HID1 // P])
        bias2 = sb("bias2", [P, HID2 // P])
        ids_all = sb("ids_all", [P, BATCH_TILES, FIELDS], int32)
        ids_now = sb("ids_now", [P, FIELDS], int32)
        gathered = sb("gathered", [P, FIELDS, WIDTH])
        embedded = sb("embedded", [P, FIELDS, BATCH_TILES * WIDTH])
        fields = sb("fields", [P, 2, TILES, FIELDS])
        early = sb("early", [P, FIELDS, TILES])
        early_t = sb("early_t", [P, P])
        repeated = sb("repeated", [P, COLS])
        pairs = sb("pairs", [P, BLOCKS, COLS])
        block_high = sb("block_high", [P, COLS], fp32r)
        block_low = sb("block_low", [P, COLS], fp32r)
        last_pairs = sb("last_pairs", [P, COLS], fp32r)
        maps_high = sb("maps_high", [P, 2, COLS], fp32r)
        maps_low = sb("maps_low", [P, 2, COLS], fp32r)
        pooled0 = gathered[:, :, :].rearrange("p f d -> p (f d)")
        lanes = sb("lanes", [P, 2, UNIT_H, COLS])
        lanes_half = sb("lanes_half", [P, 2 * COLS])
        lanes_sum = sb("lanes_sum", [P, COLS])
        scaled = sb("scaled", [P, 2, FOLD_BANKS * COLS])
        setup = scaled[:, :, :].rearrange("p j c -> p (j c)")
        pair_both = setup[:, 0:BLOCKS * 2 * MAPS].rearrange("p (t a n) -> p t a n", t=BLOCKS, a=2)
        pair_sum = setup[:, BLOCKS * 2 * MAPS:BLOCKS * 3 * MAPS].rearrange("p (t n) -> p t n", t=BLOCKS)
        last_low = setup[:, BLOCKS * 3 * MAPS:(BLOCKS * 3 + 1) * MAPS]
        extra = sb("extra", [P, 2, COLS])
        fold1 = sb("fold1", [P, 1024])
        fold2 = sb("fold2", [P, 512])
        fold3 = sb("fold3", [P, 256])
        fold4 = sb("fold4", [P, 2, COLS])
        total = sb("total", [P, COLS])
        pooled0_wide = sb("pooled0_wide", [P, BATCH_TILES * COLS])
        pooled1_wide = filter1_full
        pooled1 = sb("pooled1", [P, BATCH])
        dense_in = sb("dense_in", [P, BATCH_TILES, P])
        in_order = embedded[:, :, :].rearrange("p f c -> p (f c)")
        hidden1 = in_order[:, 0:HID1 // P * BATCH].rearrange("p (k b) -> p k b", b=BATCH)
        hidden2 = in_order[:, HID1 // P * BATCH:(HID1 + HID2) // P * BATCH].rearrange(
            "p (k b) -> p k b", b=BATCH)
        rest = in_order[:, (HID1 + HID2) // P * BATCH:]
        pooled1_t, dense_t = rest[:, 0:BATCH], rest[:, BATCH:2 * BATCH]
        y_row = pooled1[0:1, :]

        inner = [pb(f"inner{i}") for i in range(RING)]
        maps_sum = pb("maps_sum")
        turned = [pb("turned"), maps_sum]

        ids_loaded = sem("ids_loaded")
        filter0_loaded = sem("filter0_loaded")
        filter1_loaded = sem("filter1_loaded")
        top_loaded = sem("top_loaded")
        rows_gathered = sem("rows_gathered")
        embedded_ready = sem("embedded_ready")
        stored = sem("stored")
        identity_blank = sem("identity_blank")
        identity_ready = sem("identity_ready")
        match_ready = sem("match_ready")
        blanks_ready = sem("blanks_ready")
        pair_filter_ready = sem("pair_filter_ready")
        high_ready = sem("high_ready")
        low_ready = sem("low_ready")
        ids_ready = sem("ids_ready")
        fields_ready = sem("fields_ready")
        early_ready = sem("early_ready")
        fields_turned = sem("fields_turned")
        turned_copied = sem("turned_copied")
        turned_stored = sem("turned_stored")
        repeated_loaded = sem("repeated_loaded")
        moved_loaded = [sem(f"moved_loaded{t}") for t in range(BLOCKS)]
        pairs_ready = sem("pairs_ready")
        block_high_ready = sem("block_high_ready")
        block_low_ready = sem("block_low_ready")
        last_high_ready = sem("last_high_ready")
        last_low_ready = sem("last_low_ready")
        last_filter_steps = sem("last_filter_steps")
        block_contracted = sem("block_contracted")
        maps_high_ready = sem("maps_high_ready")
        maps_low_ready = sem("maps_low_ready")
        pooled0_added = sem("pooled0_added")
        inner_ready = sem("inner_ready")
        unit_added = sem("unit_added")
        bank_scaled = sem("bank_scaled")
        folded = sem("folded")
        lanes_halved = sem("lanes_halved")
        lanes_summed = sem("lanes_summed")
        pooled_folded = sem("pooled_folded")
        total_ready = sem("total_ready")
        pooled1_added = sem("pooled1_added")
        top_turned = sem("top_turned")
        top_turned_copied = sem("top_turned_copied")
        hidden_summed = sem("hidden_summed")
        hidden_ready = sem("hidden_ready")
        y_summed = sem("y_summed")
        y_ready = sem("y_ready")

        def load_pairs(queue):
            def load(block_, first, count, row, apart):
                src = bass.AP(tensor=filter0.tensor, offset=row * MAPS,
                              ap=[[(FIELDS + 1) * MAPS, count], [apart * MAPS, 2], [1, MAPS]])
                queue.dma_start(pair_both[first:first + count, block_, :, :], src).then_inc(filter0_loaded, 16)

            half = FIELDS // 2
            diagonal = bass.AP(tensor=filter0.tensor, offset=0, ap=[[(FIELDS + 1) * MAPS, FIELDS], [1, MAPS]])
            queue.dma_start(pair_both[0:FIELDS, 0, 0, :], diagonal).then_inc(filter0_loaded, 16)
            for s in range(1, half):
                at = s % DIST * FIELDS
                load(s // DIST, at, FIELDS - s, s, (FIELDS - 1) * s)
                i = FIELDS - s
                load(s // DIST, at + i, s, (FIELDS + 1) * i + FIELDS * (s - FIELDS), (FIELDS - 1) * (FIELDS - s))
            for copy in range(4):
                load(FULL, copy * half, half, half, (FIELDS - 1) * half)

        PAIR_LOADS = 1 + 2 * (FIELDS // 2 - 1) + 4

        mlp_steps = [(half, layer, o) for half in range(2) for layer, outs in ((1, HID1), (2, HID2))
                     for o in range(outs // P)]

        spare = nc.dram_tensor("spare", (2, 2 * FIELDS, COLS), fp32, kind="Internal").ap()

        block = ctx.enter_context(nc.Block())

        @block.sync
        def _(sp):
            sp.dma_start(ids_all[:, :, :], ids.rearrange("(t p) f -> p t f", p=P)).then_inc(ids_loaded, 16)
            sp.dma_start(filter1_full[:, :].rearrange("m (h n) -> m h n", h=FIELDS),
                         filter1.rearrange("o (h m) n -> m (o h) n", m=MAPS)).then_inc(filter1_loaded, 16)
            sp.wait_ge(blanks_ready, 2)
            load_pairs(sp)
            sp.wait_ge(blanks_ready, 4)
            for k in range(2):
                sp.dma_start(top1[:, k, :], w_top1[k * P:(k + 1) * P, :]).then_inc(top_loaded, 16)
            sp.dma_start(top1[0:DENSE, 2, :], w_top1[2 * P:2 * P + DENSE, :]).then_inc(top_loaded, 16)
            sp.dma_start(top2[:, :, :], w_top2.rearrange("(k p) n -> p k n", p=P)).then_inc(top_loaded, 16)
            sp.dma_start(top3[:, :], w_top3.rearrange("(k p) n -> p (k n)", p=P),
                         allow_slow_non_contiguous=True).then_inc(top_loaded, 16)
            sp.dma_start(bias1[:, :], b_top1.rearrange("(k p) -> p k", p=P),
                         allow_slow_non_contiguous=True).then_inc(top_loaded, 16)
            sp.dma_start(bias2[:, :], b_top2.rearrange("(k p) -> p k", p=P),
                         allow_slow_non_contiguous=True).then_inc(top_loaded, 16)
            sp.dma_start(dense_in[:, :, 0:DENSE],
                         dense.rearrange("(t p) f -> p t f", p=P)).then_inc(top_loaded, 16)

            def spread_group(G, par):
                base = spare[par, 0, 0:1]

                def rows(first, step, count):
                    return bass.AP(tensor=base.tensor, offset=base.offset + first * COLS,
                                   ap=[[step * COLS, count], [COLS, FIELDS], [1, COLS]])

                def write(copy):
                    sp.dma_start(spare[par, copy * FIELDS:(copy + 1) * FIELDS, :].rearrange(
                        "f (j s) -> (f j) s", s=P), early_t[:, :]).then_inc(turned_stored, 16)

                sp.wait_ge(turned_copied, G + 1)
                write(0)
                if positive(G):
                    sp.wait_ge(block_contracted, (G - 1) * BLOCKS + 1)
                write(1)
                sp.wait_ge(turned_stored, (G + 1) * 32)
                for t in range(FULL):
                    if t and positive(G):
                        sp.wait_ge(block_contracted, (G - 1) * BLOCKS + (t + 1))
                    sp.dma_start(pairs[:, t, :], rows(DIST * t, 1, DIST)).then_inc(moved_loaded[t], 16)
                if positive(G):
                    sp.wait_ge(pairs_ready, G * BLOCKS)
                sp.dma_start(repeated[:, :], rows(0, 0, DIST)).then_inc(repeated_loaded, 16)
                if positive(G):
                    sp.wait_ge(last_low_ready, G)
                sp.dma_start(pairs[0:2 * FIELDS, FULL, :], rows(DIST * FULL, 0, 2)).then_inc(moved_loaded[FULL], 16)

            def batch_tile(bt, more):
                for g in range(GROUPS_OF_BT):
                    spread_group(bt * GROUPS_OF_BT + g, g % 2)

            batch_tile(0, True)
            with sp.Fori(1, BATCH_TILES) as bt:
                sp.wait_ge(rows_gathered, (bt + 1) * (16 * FIELDS))
                sp.dma_start(embedded[:, :, bass.ds(bt * WIDTH, WIDTH)],
                             gathered[:, :, :]).then_inc(embedded_ready, 16)
                batch_tile(bt, True)
            sp.wait_ge(y_ready, 2)
            sp.dma_start(out.rearrange("b o -> o b"), y_row[0:1, :]).then_inc(stored, 16)
            sp.wait_ge(stored, 16)

        @block.gpsimd
        def _(pool):
            nc.gpsimd.memset(identity[:, :], 1.0).then_inc(identity_blank, 1)
            pool.wait_ge(identity_blank, 1)
            nc.gpsimd.affine_select(out=identity[:, :], in_=identity[:, :], compare_op=ALU.is_equal,
                                    fill=0.0, base=0, pattern=[[-1, P]],
                                    channel_multiplier=1).then_inc(identity_ready, 1)

            def next_ids(bt):
                if positive(bt):
                    pool.wait_ge(ids_ready, bt)
                nc.gpsimd.tensor_copy(ids_now[:, :], ids_all[:, bass.ds(bt, 1), :].rearrange(
                    "p t f -> p (t f)")).then_inc(ids_ready, 1)
                pool.wait_ge(ids_ready, bt + 1)

            def gather(f, landing):
                pool.indirect_dma_start(landing[:, f, 0:WIDTH], None, tables[f][:, :],
                                        bass.IndirectOffsetOnAxis(ap=ids_now[:, f:f + 1], axis=0)
                                        ).then_inc(rows_gathered, 16)

            def fold_tile(group, j, par):
                tile = group * TILES + j
                pool.wait_ge(bank_scaled, group * (TILES * ACT_BANKS) + (j + 1) * ACT_BANKS)
                if positive(tile):
                    pool.wait_ge(folded, tile * 4)
                nc.gpsimd.tensor_tensor(fold1[:, :], scaled[:, j % 2, 0:1024], scaled[:, j % 2, 1024:2048],
                                        ALU.add).then_inc(folded, 1)
                pool.wait_ge(folded, tile * 4 + 1)
                nc.gpsimd.tensor_tensor(fold2[:, :], fold1[:, 0:512], fold1[:, 512:1024],
                                        ALU.add).then_inc(folded, 1)
                pool.wait_ge(folded, tile * 4 + 2)
                nc.gpsimd.tensor_tensor(fold3[:, :], fold2[:, 0:256], fold2[:, 256:512],
                                        ALU.add).then_inc(folded, 1)
                pool.wait_ge(folded, tile * 4 + 3)
                if positive(group - 1):
                    pool.wait_ge(total_ready, group - 1)
                nc.gpsimd.tensor_tensor(fold4[:, par, j * MAPS:(j + 1) * MAPS], fold3[:, 0:MAPS],
                                        fold3[:, MAPS:2 * MAPS], ALU.add).then_inc(folded, 1)

            def batch_tile(bt, more1, more2):
                for n in range(GROUPS_OF_BT * TILES):
                    if more2 and n == FIRST_EARLY:
                        pool.wait_ge(rows_gathered, (bt + 2) * (16 * FIELDS))
                        pool.wait_ge(embedded_ready, (bt + 1) * 16)
                        next_ids(bt + 2)
                    fold_tile(bt * GROUPS_OF_BT + n // TILES, n % TILES, n // TILES % 2)
                    if more1 and n < FIELDS - EARLY_FIELDS:
                        gather(EARLY_FIELDS + n, gathered)
                    if more2 and n >= FIRST_EARLY:
                        gather(n - FIRST_EARLY, gathered)
                if more2:
                    gather(EARLY_FIELDS - 1, gathered)

            pool.wait_ge(ids_loaded, 16)
            next_ids(0)
            for f in range(FIELDS):
                gather(f, embedded)
            pool.wait_ge(rows_gathered, 16 * FIELDS)
            next_ids(1)
            for f in range(EARLY_FIELDS):
                gather(f, gathered)
            batch_tile(0, True, True)
            with pool.Fori(1, BATCH_TILES - 2) as bt:
                batch_tile(bt, True, True)
            batch_tile(BATCH_TILES - 2, True, False)
            batch_tile(BATCH_TILES - 1, False, False)

        @block.scalar
        def _(act):
            act.wait_ge(filter1_loaded, 16)
            nc.scalar.activation(filter1_high[:, :], filter1_full[:, :], ACT.Copy).then_inc(high_ready, 1)
            act.wait_ge(pair_filter_ready, 1)
            for n, t in enumerate(SPLIT):
                nc.scalar.activation(split_high[:, n, :], pair_sum[:, t, :], ACT.Copy).then_inc(high_ready, 1)
            nc.scalar.activation(last_high[:, :], pair_sum[:, FULL, :], ACT.Copy).then_inc(high_ready, 1)

            def rows_of(G):
                return embedded[:, :, bass.ds(G * TILES, TILES)].rearrange("p f j -> p j f")

            def fields_can_be_taken(G):
                if positive(G // GROUPS_OF_BT):
                    act.wait_ge(embedded_ready, G // GROUPS_OF_BT * 16)
                if positive(G - 1):
                    act.wait_ge(unit_added, (G - 1) * (TILES * DVE_UNITS))
                    act.wait_ge(bank_scaled, (G - 1) * (TILES * ACT_BANKS))

            def take_fields(G, par):
                nc.scalar.activation(fields[:, par, :, :], rows_of(G), ACT.Copy).then_inc(fields_ready, 1)

            def early_can_be_taken(G):
                if positive(G // GROUPS_OF_BT):
                    act.wait_ge(embedded_ready, G // GROUPS_OF_BT * 16)
                if positive(G):
                    act.wait_ge(fields_turned, G)

            def take_early(G):
                nc.scalar.activation(early[:, :, :], embedded[:, :, bass.ds(G * TILES, TILES)],
                                     ACT.Copy).then_inc(early_ready, 1)

            def take_block_high(G, t):
                act.wait_ge(pairs_ready, G * BLOCKS + (t + 1))
                if positive(split_used(G, t)):
                    act.wait_ge(block_contracted, split_used(G, t))
                nc.scalar.activation(block_high[:, :], pairs[:, t, :], ACT.Copy).then_inc(block_high_ready, 1)

            def take_last_high(G):
                act.wait_ge(pairs_ready, (G + 1) * BLOCKS)
                if positive(G):
                    act.wait_ge(block_contracted, G * BLOCKS)
                nc.scalar.activation(last_pairs[0:2 * FIELDS, :], pairs[0:2 * FIELDS, FULL, :],
                                     ACT.Copy).then_inc(last_high_ready, 1)

            def take_turned(G):
                act.wait_ge(fields_turned, G + 1)
                if positive(G):
                    act.wait_ge(turned_stored, G * 32)
                nc.scalar.activation(early_t[:, :], turned[0][:, 0:P], ACT.Copy).then_inc(turned_copied, 1)

            def take_maps(G, par):
                act.wait_ge(block_contracted, (G + 1) * BLOCKS)
                if positive(G - 1):
                    act.wait_ge(inner_ready, (G - 1) * SLOTS)
                nc.scalar.activation(maps_high[:, par, :], maps_sum[:, :],
                                     ACT.Relu).then_inc(maps_high_ready, 1)

            def group(G, par, more1, more2):
                for k in range(SLOTS):
                    j, b = k // FILLS, k % FILLS
                    if OWNER[b] == "V":
                        continue
                    if b == 0 and positive(G * TILES + (j - 1)):
                        act.wait_ge(folded, G * (TILES * 4) + ((j - 2) * 4 + 1))
                        act.wait_ge(unit_added, G * (TILES * DVE_UNITS) + ((j - 2) * DVE_UNITS + UNIT_H))
                    if more1 and k == FIELDS_AFTER:
                        fields_can_be_taken(G + 1)
                    if more2 and k == EARLY_AFTER:
                        early_can_be_taken(G + 2)
                    act.wait_ge(inner_ready, G * SLOTS + (k + 1))
                    for c in range(UNIT_H):
                        h = b * UNIT_H + c
                        if OWNER[b] == "X":
                            dst = extra[:, j % 2, c * MAPS:(c + 1) * MAPS]
                        else:
                            at = OWNER[:b].count("S") * COLS + c * MAPS
                            dst = scaled[:, j % 2, at:at + MAPS]
                        last = nc.scalar.activation(dst, inner[bank_of(k)][:, c * MAPS:(c + 1) * MAPS],
                                                    ACT.Copy, scale=fields[:, par, j, h:h + 1])
                    last.then_inc(bank_scaled, 1)
                    if more1 and k == FIELDS_AFTER:
                        take_fields(G + 1, 1 - par)
                    if more1 and k == LAST_HIGH_AFTER:
                        take_last_high(G + 1)
                    if more1 and k == MAPS_AFTER:
                        take_maps(G + 1, 1 - par)
                    if more2 and k == BLOCK_HIGH_AFTER[0]:
                        take_block_high(G + 2, 0)
                    if more1 and k in BLOCK_HIGH_AFTER[1:]:
                        take_block_high(G + 1, SPLIT[BLOCK_HIGH_AFTER.index(k)])
                    if more2 and k == EARLY_AFTER:
                        take_early(G + 2)
                    if more2 and k == TURNED_AFTER:
                        take_turned(G + 2)

            act.wait_ge(rows_gathered, 16 * FIELDS)
            take_early(0)
            take_fields(0, 0)
            take_turned(0)
            early_can_be_taken(1)
            take_early(1)
            take_turned(1)
            for t in SPLIT:
                take_block_high(0, t)
            take_last_high(0)
            take_maps(0, 0)
            take_block_high(1, 0)
            group(0, 0, True, True)
            group(1, 1, True, True)
            with act.Fori(1, GROUPS // 2 - 1) as pair:
                group(pair * 2, 0, True, True)
                group(pair * 2 + 1, 1, True, True)
            group(GROUPS - 2, 0, True, False)
            group(GROUPS - 1, 1, False, False)

            act.wait_ge(top_loaded, 16 * 8)
            for n, (half, layer, o) in enumerate(mlp_steps):
                act.wait_ge(hidden_summed, n + 1)
                dst, bias = (hidden1, bias1) if layer == 1 else (hidden2, bias2)
                nc.scalar.activation(dst[:, o, half * 512:(half + 1) * 512], inner[n % RING][:, :],
                                     ACT.Relu, bias=bias[:, o:o + 1]).then_inc(hidden_ready, 1)
            for half in range(2):
                act.wait_ge(y_summed, half + 1)
                nc.scalar.activation(y_row[0:1, half * 512:(half + 1) * 512], turned[half][0:1, :],
                                     ACT.Copy).then_inc(y_ready, 1)

        @block.vector
        def _(dve):
            nc.vector.memset(pair_both[:, 0, 1, :], 0.0).then_inc(blanks_ready, 1)
            nc.vector.memset(pair_both[:, FULL, :, :], 0.0).then_inc(blanks_ready, 1)
            dve.wait_ge(identity_ready, 1)
            nc.vector.tensor_reduce(field_match[:, :], identity[:, :].rearrange("p (q f) -> p f q", f=FIELDS),
                                    AX.X, ALU.add).then_inc(match_ready, 1)
            dve.wait_ge(match_ready, 1)
            nc.vector.tensor_reduce(takes_high[:, :], field_match[:, 0:FIELDS // 2], AX.X,
                                    ALU.add).then_inc(last_filter_steps, 1)
            nc.vector.tensor_reduce(takes_low[:, :], field_match[:, FIELDS // 2:FIELDS], AX.X,
                                    ALU.add).then_inc(last_filter_steps, 1)
            nc.vector.memset(dense_in[:, :, :], 0.0).then_inc(blanks_ready, 1)
            nc.vector.memset(top1[:, 2, :], 0.0).then_inc(blanks_ready, 1)
            nc.vector.memset(last_pairs[2 * FIELDS:P, :].bitcast(fp32), 0.0).then_inc(last_filter_steps, 1)
            nc.vector.memset(pooled0_wide[:, :], 0.0).then_inc(pooled0_added, 1)
            dve.wait_ge(high_ready, 1)
            nc.vector.tensor_tensor(filter1_low[:, :], filter1_full[:, :],
                                    filter1_high[:, :].bitcast(fp32), ALU.subtract).then_inc(low_ready, 1)
            dve.wait_ge(low_ready, 1)
            nc.vector.memset(pooled1_wide[:, :], 0.0).then_inc(pooled1_added, 1)
            dve.wait_ge(filter0_loaded, 16 * PAIR_LOADS)
            nc.vector.tensor_tensor(pair_sum[:, :, :], pair_both[:, :, 0, :], pair_both[:, :, 1, :],
                                    ALU.add).then_inc(pair_filter_ready, 1)
            for n, t in enumerate(KEPT):
                nc.vector.tensor_tensor(pair_filter[:, n, :], pair_both[:, t, 0, :], pair_both[:, t, 1, :],
                                        ALU.add).then_inc(pair_filter_ready, 1)
            dve.wait_ge(pair_filter_ready, 1)
            for n, t in enumerate(SPLIT):
                dve.wait_ge(high_ready, 2 + n)
                nc.vector.tensor_tensor(split_low[:, n, :], pair_sum[:, t, :],
                                        split_high[:, n, :].bitcast(fp32), ALU.subtract).then_inc(low_ready, 1)
            dve.wait_ge(high_ready, 2 + len(SPLIT))
            nc.vector.tensor_tensor(last_low[:, :], pair_sum[:, FULL, :], last_high[:, :].bitcast(fp32),
                                    ALU.subtract).then_inc(last_filter_steps, 1)
            dve.wait_ge(last_filter_steps, 4)
            nc.vector.tensor_scalar(last_low[:, :], last_low[:, :], takes_low[:, 0:1], None,
                                    ALU.mult).then_inc(last_filter_steps, 1)
            dve.wait_ge(last_filter_steps, 5)
            nc.vector.scalar_tensor_tensor(out=last_filter[:, :], in0=last_high[:, :].bitcast(fp32),
                                           scalar=takes_high[:, 0:1], in1=last_low[:, :],
                                           op0=ALU.mult, op1=ALU.add).then_inc(last_filter_steps, 1)

            def make_pairs(G, t):
                rows = slice(0, P if t < FULL else 2 * FIELDS)
                dve.wait_ge(repeated_loaded, (G + 1) * 16)
                dve.wait_ge(moved_loaded[t], (G + 1) * 16)
                nc.vector.tensor_tensor(pairs[rows, t, :], pairs[rows, t, :], repeated[rows, :],
                                        ALU.mult).then_inc(pairs_ready, 1)

            def take_block_low(G, t):
                dve.wait_ge(block_high_ready, G * len(SPLIT) + (SPLIT.index(t) + 1))
                if positive(split_used(G, t)):
                    dve.wait_ge(block_contracted, split_used(G, t))
                nc.vector.tensor_tensor(block_low[:, :], pairs[:, t, :], block_high[:, :].bitcast(fp32),
                                        ALU.subtract).then_inc(block_low_ready, 1)

            def take_last_low(G):
                dve.wait_ge(last_high_ready, G + 1)
                rows = slice(FIELDS, 2 * FIELDS)
                nc.vector.tensor_tensor(last_pairs[rows, :], pairs[rows, FULL, :],
                                        last_pairs[rows, :].bitcast(fp32), ALU.subtract).then_inc(last_low_ready, 1)

            def split_maps(G, par):
                dve.wait_ge(maps_high_ready, G + 1)
                nc.vector.scalar_tensor_tensor(out=maps_low[:, par, :], in0=maps_sum[:, :], scalar=0.0,
                                               in1=maps_high[:, par, :].bitcast(fp32), op0=ALU.max,
                                               op1=ALU.subtract).then_inc(maps_low_ready, 1)

            def pool_maps(G):
                dve.wait_ge(maps_high_ready, G + 1)
                dve.wait_ge(pooled0_added, G + 1)
                acc = pooled0_wide[:, bass.ds(G // GROUPS_OF_BT * COLS, COLS)]
                nc.vector.scalar_tensor_tensor(out=acc, in0=maps_sum[:, :], scalar=0.0, in1=acc,
                                               op0=ALU.max, op1=ALU.add).then_inc(pooled0_added, 1)

            def halve_lanes(G, par):
                dve.wait_ge(unit_added, (G + 1) * (TILES * DVE_UNITS))
                nc.vector.tensor_tensor(lanes_half[:, :].rearrange("p (a n) -> p a n", a=2),
                                        lanes[:, par, 0:2, :], lanes[:, par, 2:4, :],
                                        ALU.add).then_inc(lanes_halved, 1)

            def sum_lanes(G):
                dve.wait_ge(lanes_halved, G + 1)
                nc.vector.tensor_tensor(lanes_sum[:, :], lanes_half[:, 0:COLS], lanes_half[:, COLS:2 * COLS],
                                        ALU.add).then_inc(lanes_summed, 1)

            def sum_total(G, par):
                dve.wait_ge(lanes_summed, G + 1)
                dve.wait_ge(folded, (G + 1) * (TILES * 4))
                nc.vector.tensor_tensor(total[:, :], lanes_sum[:, :], fold4[:, par, :],
                                        ALU.add).then_inc(total_ready, 1)

            def pool_total(G):
                dve.wait_ge(total_ready, G + 1)
                dve.wait_ge(pooled1_added, G + 1)
                acc = pooled1_wide[:, bass.ds(G // GROUPS_OF_BT * COLS, COLS)]
                nc.vector.scalar_tensor_tensor(out=acc, in0=total[:, :], scalar=0.0, in1=acc,
                                               op0=ALU.max, op1=ALU.add).then_inc(pooled1_added, 1)

            def group(G, par, more1, more2, folds=(), fold=None):
                folds = list(folds)
                for k in range(SLOTS):
                    j, b = k // FILLS, k % FILLS
                    if OWNER[b] != "V":
                        continue
                    n_before = OWNER[:b].count("V") * UNIT_H
                    if n_before == 0:
                        dve.wait_ge(bank_scaled, G * (TILES * ACT_BANKS) + (j * ACT_BANKS + 1))
                        if positive(G - 1):
                            dve.wait_ge(lanes_halved, G - 1)
                    dve.wait_ge(inner_ready, G * SLOTS + (k + 1))
                    for c in range(UNIT_H):
                        h = b * UNIT_H + c
                        acc = lanes[:, par, c, j * MAPS:(j + 1) * MAPS]
                        before = extra[:, j % 2, c * MAPS:(c + 1) * MAPS] if n_before == 0 else acc
                        if n_before:
                            dve.wait_ge(unit_added, G * (TILES * DVE_UNITS)
                                        + (j * DVE_UNITS + n_before + c - UNIT_H + 1))
                        nc.vector.scalar_tensor_tensor(out=acc, in0=inner[bank_of(k)][:, c * MAPS:(c + 1) * MAPS],
                                                       scalar=fields[:, par, j, h:h + 1], in1=before,
                                                       op0=ALU.mult, op1=ALU.add).then_inc(unit_added, 1)
                    if folds and k not in (LANES_AFTER, LANES_SUM_AFTER, TOTAL_AFTER, POOL_TOTAL_AFTER):
                        wide, narrow, bt = folds.pop(0)
                        fold(wide, narrow, bt, bt + 1)
                    if positive(G) and k == LANES_AFTER:
                        halve_lanes(G - 1, 1 - par)
                    if positive(G) and k == LANES_SUM_AFTER:
                        sum_lanes(G - 1)
                    if positive(G) and k == TOTAL_AFTER:
                        sum_total(G - 1, 1 - par)
                    if positive(G) and k == POOL_TOTAL_AFTER:
                        pool_total(G - 1)
                    if more1 and k in PAIRS_AFTER[1:]:
                        make_pairs(G + 1, PAIRS_AFTER.index(k))
                    if more2 and k == BLOCK_LOW_AFTER[0]:
                        take_block_low(G + 2, 0)
                    if more1 and k in BLOCK_LOW_AFTER[1:]:
                        take_block_low(G + 1, SPLIT[BLOCK_LOW_AFTER.index(k)])
                    if more1 and k == LAST_LOW_AFTER:
                        take_last_low(G + 1)
                    if more1 and k == SPLIT_AFTER:
                        split_maps(G + 1, 1 - par)
                    if k == POOL_MAPS_AFTER:
                        pool_maps(G)
                    if more2 and k == PAIRS_AFTER[0]:
                        make_pairs(G + 2, 0)

            for t in range(BLOCKS):
                make_pairs(0, t)
                if t in SPLIT:
                    take_block_low(0, t)
            take_last_low(0)
            split_maps(0, 0)
            make_pairs(1, 0)
            take_block_low(1, 0)
            group(0, 0, True, True)
            group(1, 1, True, True)
            with dve.Fori(1, GROUPS // 2 - 1) as pair:
                group(pair * 2, 0, True, True)
                group(pair * 2 + 1, 1, True, True)

            def fold_pooled(wide, narrow, first, end):
                v = wide[:, first * COLS:end * COLS].rearrange("p (t j n) -> p t n j", j=TILES, n=P)
                nc.vector.tensor_reduce(narrow[:, first * P:end * P].rearrange("p (t n) -> p t n", n=P), v,
                                        AX.X, ALU.add).then_inc(pooled_folded, 1)

            def copy_turned(half):
                for src, dst in ((0, pooled1_t), (1, dense_t)):
                    dve.wait_ge(top_turned, half * 2 + src + 1)
                    nc.vector.tensor_copy(dst[:, half * 512:(half + 1) * 512],
                                          turned[src][:, :]).then_inc(top_turned_copied, 1)

            group(GROUPS - 2, 0, True, False)
            dve.wait_ge(pooled0_added, GROUPS)
            half_tiles = BATCH_TILES // 2
            group(GROUPS - 1, 1, False, False,
                  [(wide, narrow, bt) for wide, narrow in ((pooled0_wide, pooled0), (pooled1_wide, pooled1))
                   for bt in range(half_tiles)], fold_pooled)
            copy_turned(0)
            halve_lanes(GROUPS - 1, 1)
            dve.wait_ge(pooled0_added, GROUPS + 1)
            fold_pooled(pooled0_wide, pooled0, half_tiles, BATCH_TILES)
            sum_lanes(GROUPS - 1)
            fold_pooled(pooled1_wide, pooled1, half_tiles, BATCH_TILES - 1)
            sum_total(GROUPS - 1, 1)
            pool_total(GROUPS - 1)
            dve.wait_ge(pooled1_added, GROUPS + 1)
            fold_pooled(pooled1_wide, pooled1, BATCH_TILES - 1, BATCH_TILES)
            copy_turned(1)

        @block.tensor
        def _(pe):
            def turn_fields(G):
                pe.wait_ge(early_ready, G + 1)
                if positive(G):
                    pe.wait_ge(turned_copied, G)
                nc.tensor.transpose(turned[0][:, 0:P], early[:, :, :].rearrange("p f j -> p (f j)"),
                                    identity[:, :]).then_inc(fields_turned, 1)

            def contract(G, t):
                if t == 0 and positive(G):
                    pe.wait_ge(maps_low_ready, G)
                    pe.wait_ge(pooled0_added, G + 1)
                if t in SPLIT:
                    n = SPLIT.index(t)
                    pe.wait_ge(block_low_ready, G * len(SPLIT) + (SPLIT.index(t) + 1))
                    nc.tensor.matmul(maps_sum[:, :], split_high[:, n, :], block_low[:, :],
                                     start=(t == 0), stop=False)
                    nc.tensor.matmul(maps_sum[:, :], split_low[:, n, :], block_high[:, :],
                                     start=False, stop=False)
                    last = nc.tensor.matmul(maps_sum[:, :], split_high[:, n, :], block_high[:, :],
                                            start=False, stop=False)
                else:
                    pe.wait_ge(pairs_ready, G * BLOCKS + (t + 1))
                    last = nc.tensor.matmul(maps_sum[:, :], pair_filter[:, KEPT.index(t), :], pairs[:, t, :],
                                            start=(t == 0), stop=False)
                last.then_inc(block_contracted, 1)

            def contract_last(G):
                pe.wait_ge(last_low_ready, G + 1)
                nc.tensor.matmul(maps_sum[:, :], last_filter[:, :], last_pairs[:, :], start=False,
                                 stop=True).then_inc(block_contracted, 1)

            def group(G, par, more1, more2):
                pe.wait_ge(maps_low_ready, G + 1)
                for k in range(SLOTS):
                    j, b = k // FILLS, k % FILLS
                    if more1 and k in CONTRACT_AT[:FULL]:
                        contract(G + 1, CONTRACT_AT.index(k))
                    if more1 and k == CONTRACT_AT[FULL]:
                        contract_last(G + 1)
                    if more2 and k == TURN_AT:
                        turn_fields(G + 2)
                    if OWNER[b] == "V":
                        used = slots_of("V", k) - V_RING + 1
                        if positive(G * SLOTS + used):
                            pe.wait_ge(unit_added, (G * (TILES * DVE_UNITS) + used * UNIT_H))
                    else:
                        used = slots_of("SX", k) - S_RING + 1
                        if positive(G * SLOTS + used):
                            pe.wait_ge(bank_scaled, G * (TILES * ACT_BANKS) + used)
                    high = maps_high[:, par, j * P:(j + 1) * P]
                    low = maps_low[:, par, j * P:(j + 1) * P]
                    cols = slice(b * COLS, (b + 1) * COLS)
                    y = inner[bank_of(k)]
                    nc.tensor.matmul(y[:, :], low, filter1_high[:, cols], start=True, stop=False)
                    nc.tensor.matmul(y[:, :], high, filter1_low[:, cols], start=False, stop=False)
                    nc.tensor.matmul(y[:, :], high, filter1_high[:, cols], start=False,
                                     stop=True).then_inc(inner_ready, 1)

            pe.wait_ge(identity_ready, 1)
            turn_fields(0)
            turn_fields(1)
            pe.wait_ge(pair_filter_ready, 1 + len(KEPT))
            pe.wait_ge(low_ready, 1 + len(SPLIT))
            for t in range(FULL):
                contract(0, t)
            pe.wait_ge(last_filter_steps, 6)
            contract_last(0)
            group(0, 0, True, True)
            group(1, 1, True, True)
            with pe.Fori(1, GROUPS // 2 - 1) as pair:
                group(pair * 2, 0, True, True)
                group(pair * 2 + 1, 1, True, True)
            group(GROUPS - 2, 0, True, False)
            group(GROUPS - 1, 1, False, False)

            pe.wait_ge(top_loaded, 16 * 8)
            pe.wait_ge(unit_added, GROUPS * TILES * DVE_UNITS)
            pe.wait_ge(bank_scaled, GROUPS * TILES * ACT_BANKS)
            for half in range(2):
                pe.wait_ge(pooled_folded, 8 + 3 * half)
                if half:
                    pe.wait_ge(top_turned_copied, 2)
                for src in range(2):
                    for j in range(TILES):
                        bt = half * TILES + j
                        a = pooled1[:, bt * P:(bt + 1) * P] if src == 0 else dense_in[:, bt, :]
                        last = nc.tensor.transpose(turned[src][:, j * P:(j + 1) * P], a, identity[:, :])
                    last.then_inc(top_turned, 1)
                pe.wait_ge(top_turned_copied, 2 * (half + 1))
                cols = slice(half * 512, (half + 1) * 512)
                for n, (of_half, layer, o) in enumerate(mlp_steps):
                    if of_half != half:
                        continue
                    if n >= RING:
                        pe.wait_ge(hidden_ready, n - RING + 1)
                    if layer == 1:
                        terms = [(top1[:, k, o * P:(o + 1) * P], rhs[:, cols])
                                 for k, rhs in enumerate((pooled0, pooled1_t, dense_t))]
                    else:
                        pe.wait_ge(hidden_ready, n - o)
                        terms = [(top2[:, k, o * P:(o + 1) * P], hidden1[:, k, cols]) for k in range(HID1 // P)]
                    for k, (w, x) in enumerate(terms):
                        last = nc.tensor.matmul(inner[n % RING][:, :], w, x, start=(k == 0),
                                                stop=(k == len(terms) - 1))
                    last.then_inc(hidden_summed, 1)
            for half in range(2):
                pe.wait_ge(hidden_ready, len(mlp_steps) // 2 * (half + 1))
                for k in range(HID2 // P):
                    last = nc.tensor.matmul(turned[half][0:1, :], top3[:, k:k + 1],
                                            hidden2[:, k, half * 512:(half + 1) * 512],
                                            start=(k == 0), stop=(k == HID2 // P - 1))
                last.then_inc(y_summed, 1)


_INS = (["dense_ctx", "ids"] + [f"tbl_{f}" for f in range(FIELDS)]
        + ["W_top1", "b_top1", "W_top2", "b_top2", "W_top3", "L0_rec_filter_0", "L0_rec_filter_1"])


def kernel(**inputs):
    import numpy as _np
    import concourse.bacc as _bacc
    from concourse import mybir as _mybir
    from concourse.bass_utils import run_bass_kernel_spmd as _run

    nc = _bacc.Bacc("TRN2", target_bir_lowering=False, num_devices=1)
    arrays, ap = {}, {}
    for name in _INS:
        a = _np.ascontiguousarray(inputs[name])
        arrays[f"in_{name}"] = a
        ap[name] = nc.dram_tensor(f"in_{name}", a.shape, _mybir.dt.from_np(a.dtype), kind="ExternalInput").ap()
    out = nc.dram_tensor("out_y", (BATCH, 1), _mybir.dt.float32, kind="ExternalOutput").ap()
    dlrm_tower(nc, ap["dense_ctx"], ap["ids"], [ap[f"tbl_{f}"] for f in range(FIELDS)], ap["W_top1"],
               ap["b_top1"], ap["W_top2"], ap["b_top2"], ap["W_top3"], ap["L0_rec_filter_0"],
               ap["L0_rec_filter_1"], out)
    r = _run(nc, [arrays], core_ids=[0])
    return r.results[0]["out_y"]
```

```python
import concourse.bass as bass
from concourse import mybir
from contextlib import ExitStack

BATCH, FIELDS, WIDTH, MAPS = 1024, 32, 32, 128
DENSE, HID1, HID2 = 16, 512, 256
P = 128
BATCH_TILES = BATCH // P
TILES = 4
GROUPS_OF_BT = WIDTH // TILES
GROUPS = BATCH_TILES * GROUPS_OF_BT
COLS = TILES * P
DIST = P // FIELDS
BLOCKS = 5
FULL = BLOCKS - 1
UNIT_H = COLS // MAPS
FILLS = FIELDS // UNIT_H
SLOTS = TILES * FILLS
EARLY_TILES, EARLY_FIELDS = 8, 10
FIRST_EARLY = GROUPS_OF_BT * TILES - EARLY_TILES
V_RING, S_RING = 2, 4
RING = V_RING + S_RING
OWNER = "XSVSSVSV"
DVE_UNITS = OWNER.count("V") * UNIT_H
ACT_BANKS = FILLS - OWNER.count("V")
FOLD_BANKS = OWNER.count("S")
FOLDS = TILES * 3 + 1
CONTRACT_AT = [8, 12, 19, 24, 25]
TURN_AT = 16
BLOCK_HIGH_AFTER = [30, 4, 12, 17]
FIELDS_AFTER, LAST_HIGH_AFTER, MAPS_AFTER = 6, 19, 25
EARLY_AFTER, TURNED_AFTER = 11, 17
PAIRS_AFTER = [29, 2, 10, 15, 18]
BLOCK_LOW_AFTER = [31, 5, 13, 18]
LAST_LOW_AFTER, SPLIT_AFTER, POOL_MAPS_AFTER = 21, 26, 2
LANES_AFTER, LANES_SUM_AFTER, TOTAL_AFTER, POOL_TOTAL_AFTER = 7, 13, 23, 23
HALF_FOLD_AFTER = [2, 5, 10, 15]
HALF_TURN_AT, HALF_COPY_AFTER = 21, 26


def slots_of(owners, end):
    return sum(OWNER[k % FILLS] in owners for k in range(end))


def bank_of(k):
    if OWNER[k % FILLS] == "V":
        return slots_of("V", k) % V_RING
    return V_RING + slots_of("SX", k) % S_RING


def place_free_after(G, t):
    return G * BLOCKS + (t - 1 if t >= 2 else t + 2 - BLOCKS)


def positive(count):
    return not isinstance(count, int) or count > 0


def dlrm_tower(nc, dense, ids, tables, w_top1, b_top1, w_top2, b_top2, w_top3, filter0, filter1, out):
    fp32, fp32r, int32 = mybir.dt.float32, mybir.dt.float32r, mybir.dt.int32
    ALU, ACT, AX = mybir.AluOpType, mybir.ActivationFunctionType, mybir.AxisListType

    with ExitStack() as ctx:
        def sb(name, shape, dt=fp32):
            return ctx.enter_context(nc.sbuf_tensor(name, shape, dt))

        def pb(name, dt=fp32):
            return ctx.enter_context(nc.psum_tensor(name, [P, COLS], dt))

        def sem(name):
            return ctx.enter_context(nc.semaphore(name))

        identity = sb("identity", [P, P])
        field_match = sb("field_match", [P, FIELDS])
        filter0_high = sb("filter0_high", [P, FULL, MAPS], fp32r)
        filter0_low = sb("filter0_low", [P, FULL, MAPS], fp32r)
        last_filter = sb("last_filter", [P, MAPS], fp32r)
        takes_high = sb("takes_high", [P, 1])
        takes_low = sb("takes_low", [P, 1])
        filter1_full = sb("filter1_full", [P, FIELDS * MAPS])
        filter1_high = sb("filter1_high", [P, FIELDS * MAPS], fp32r)
        filter1_low = sb("filter1_low", [P, FIELDS * MAPS], fp32r)
        top1 = sb("top1", [P, 3, HID1])
        top2 = sb("top2", [P, HID1 // P, HID2])
        top3 = sb("top3", [P, HID2 // P])
        bias1 = sb("bias1", [P, HID1 // P])
        bias2 = sb("bias2", [P, HID2 // P])
        ids_all = sb("ids_all", [P, BATCH_TILES, FIELDS], int32)
        ids_now = sb("ids_now", [P, FIELDS], int32)
        gathered = sb("gathered", [P, FIELDS, WIDTH])
        embedded = sb("embedded", [P, FIELDS, BATCH_TILES * WIDTH])
        fields = sb("fields", [P, 2, TILES, FIELDS])
        early = sb("early", [P, FIELDS, TILES])
        early_t = sb("early_t", [P, P])
        repeated = sb("repeated", [P, COLS])
        pairs = sb("pairs", [P, BLOCKS, COLS])
        pooled1 = pairs[:, 0:2, :].rearrange("p t c -> p (t c)")
        block_high = sb("block_high", [P, 2, COLS], fp32r)
        block_low = sb("block_low", [P, 2, COLS], fp32r)
        last_pairs = sb("last_pairs", [P, COLS], fp32r)
        maps_high = sb("maps_high", [P, 2, COLS], fp32r)
        maps_low = sb("maps_low", [P, 2, COLS], fp32r)
        pooled0 = gathered[:, :, :].rearrange("p f d -> p (f d)")
        lanes = sb("lanes", [P, 2, UNIT_H, COLS])
        lanes_half = sb("lanes_half", [P, 2 * COLS])
        lanes_sum = sb("lanes_sum", [P, COLS])
        scaled = sb("scaled", [P, 2, FOLD_BANKS * COLS])
        extra = sb("extra", [P, 2, COLS])
        fold1 = sb("fold1", [P, 1024])
        fold2 = sb("fold2", [P, 512])
        fold3 = sb("fold3", [P, TILES, 256])
        fold4 = sb("fold4", [P, COLS])
        total = lanes_half[:, 0:COLS]
        pooled0_wide = sb("pooled0_wide", [P, BATCH_TILES * COLS])
        pooled1_wide = filter1_full
        setup = scaled[:, :, :].rearrange("p j c -> p (j c)")
        pair_both = setup[:, 0:BLOCKS * 2 * MAPS].rearrange("p (t a n) -> p t a n", t=BLOCKS, a=2)
        pair_sum = setup[:, BLOCKS * 2 * MAPS:BLOCKS * 3 * MAPS].rearrange("p (t n) -> p t n", t=BLOCKS)
        last_low = setup[:, BLOCKS * 3 * MAPS:(BLOCKS * 3 + 1) * MAPS]
        last_high = fold1[:, 0:MAPS]
        dense_in = sb("dense_in", [P, BATCH_TILES, P])
        in_order = embedded[:, :, :].rearrange("p f c -> p (f c)")
        hidden1 = in_order[:, 0:HID1 // P * BATCH].rearrange("p (k b) -> p k b", b=BATCH)
        hidden2 = in_order[:, HID1 // P * BATCH:(HID1 + HID2) // P * BATCH].rearrange(
            "p (k b) -> p k b", b=BATCH)
        rest = in_order[:, (HID1 + HID2) // P * BATCH:]
        pooled1_t, dense_t = rest[:, 0:BATCH], rest[:, BATCH:2 * BATCH]
        y_row = pooled1[0:1, :]

        inner = [pb(f"inner{i}") for i in range(RING)]
        maps_sum = pb("maps_sum")
        turned = [pb("turned"), maps_sum]

        ids_loaded = sem("ids_loaded")
        filter0_loaded = sem("filter0_loaded")
        filter1_loaded = sem("filter1_loaded")
        top_loaded = sem("top_loaded")
        rows_gathered = sem("rows_gathered")
        embedded_ready = sem("embedded_ready")
        stored = sem("stored")
        identity_blank = sem("identity_blank")
        identity_ready = sem("identity_ready")
        match_ready = sem("match_ready")
        blanks_ready = sem("blanks_ready")
        pair_sum_ready = sem("pair_sum_ready")
        high_ready = sem("high_ready")
        low_ready = sem("low_ready")
        ids_ready = sem("ids_ready")
        fields_ready = sem("fields_ready")
        early_ready = sem("early_ready")
        fields_turned = sem("fields_turned")
        turned_copied = sem("turned_copied")
        turned_stored = sem("turned_stored")
        repeated_loaded = sem("repeated_loaded")
        moved_loaded = [sem(f"moved_loaded{t}") for t in range(BLOCKS)]
        pairs_ready = sem("pairs_ready")
        block_high_ready = sem("block_high_ready")
        block_low_ready = sem("block_low_ready")
        last_high_ready = sem("last_high_ready")
        last_low_ready = sem("last_low_ready")
        last_filter_steps = sem("last_filter_steps")
        block_contracted = sem("block_contracted")
        maps_high_ready = sem("maps_high_ready")
        maps_low_ready = sem("maps_low_ready")
        pooled0_added = sem("pooled0_added")
        inner_ready = sem("inner_ready")
        unit_added = sem("unit_added")
        bank_scaled = sem("bank_scaled")
        folded = sem("folded")
        lanes_halved = sem("lanes_halved")
        lanes_summed = sem("lanes_summed")
        pooled_folded = sem("pooled_folded")
        total_ready = sem("total_ready")
        pooled1_added = sem("pooled1_added")
        top_turned = sem("top_turned")
        top_turned_copied = sem("top_turned_copied")
        hidden_summed = sem("hidden_summed")
        hidden_ready = sem("hidden_ready")
        y_summed = sem("y_summed")
        y_ready = sem("y_ready")

        def load_pairs(queue):
            def load(block_, first, count, row, apart):
                src = bass.AP(tensor=filter0.tensor, offset=row * MAPS,
                              ap=[[(FIELDS + 1) * MAPS, count], [apart * MAPS, 2], [1, MAPS]])
                queue.dma_start(pair_both[first:first + count, block_, :, :], src).then_inc(filter0_loaded, 16)

            half = FIELDS // 2
            diagonal = bass.AP(tensor=filter0.tensor, offset=0, ap=[[(FIELDS + 1) * MAPS, FIELDS], [1, MAPS]])
            queue.dma_start(pair_both[0:FIELDS, 0, 0, :], diagonal).then_inc(filter0_loaded, 16)
            for s in range(1, half):
                at = s % DIST * FIELDS
                load(s // DIST, at, FIELDS - s, s, (FIELDS - 1) * s)
                i = FIELDS - s
                load(s // DIST, at + i, s, (FIELDS + 1) * i + FIELDS * (s - FIELDS), (FIELDS - 1) * (FIELDS - s))
            for copy in range(4):
                load(FULL, copy * half, half, half, (FIELDS - 1) * half)

        PAIR_LOADS = 1 + 2 * (FIELDS // 2 - 1) + 4

        mlp_steps = [(half, layer, o) for layer, outs in ((1, HID1), (2, HID2)) for half in range(2)
                     for o in range(outs // P)]

        def steps_through(half, layer):
            return max(n + 1 for n, (h, l, _) in enumerate(mlp_steps) if (h, l) == (half, layer))

        wrapped_fields = nc.dram_tensor("wrapped_fields", (2, 2 * FIELDS, COLS), fp32, kind="Internal").ap()

        block = ctx.enter_context(nc.Block())

        @block.sync
        def _(sp):
            sp.dma_start(ids_all[:, :, :], ids.rearrange("(t p) f -> p t f", p=P)).then_inc(ids_loaded, 16)
            sp.dma_start(filter1_full[:, :].rearrange("m (h n) -> m h n", h=FIELDS),
                         filter1.rearrange("o (h m) n -> m (o h) n", m=MAPS)).then_inc(filter1_loaded, 16)
            sp.wait_ge(blanks_ready, 2)
            load_pairs(sp)
            sp.wait_ge(blanks_ready, 4)
            for k in range(2):
                sp.dma_start(top1[:, k, :], w_top1[k * P:(k + 1) * P, :]).then_inc(top_loaded, 16)
            sp.dma_start(top1[0:DENSE, 2, :], w_top1[2 * P:2 * P + DENSE, :]).then_inc(top_loaded, 16)
            sp.dma_start(top2[:, :, :], w_top2.rearrange("(k p) n -> p k n", p=P)).then_inc(top_loaded, 16)
            sp.dma_start(top3[:, :], w_top3.rearrange("(k p) n -> p (k n)", p=P),
                         allow_slow_non_contiguous=True).then_inc(top_loaded, 16)
            sp.dma_start(bias1[:, :], b_top1.rearrange("(k p) -> p k", p=P),
                         allow_slow_non_contiguous=True).then_inc(top_loaded, 16)
            sp.dma_start(bias2[:, :], b_top2.rearrange("(k p) -> p k", p=P),
                         allow_slow_non_contiguous=True).then_inc(top_loaded, 16)
            sp.dma_start(dense_in[:, :, 0:DENSE],
                         dense.rearrange("(t p) f -> p t f", p=P)).then_inc(top_loaded, 16)

            def spread_group(G, par):
                base = wrapped_fields[par, 0, 0:1]

                def rows(first, step, count):
                    return bass.AP(tensor=base.tensor, offset=base.offset + first * COLS,
                                   ap=[[step * COLS, count], [COLS, FIELDS], [1, COLS]])

                def write(copy):
                    sp.dma_start(wrapped_fields[par, copy * FIELDS:(copy + 1) * FIELDS, :].rearrange(
                        "f (j s) -> (f j) s", s=P), early_t[:, :]).then_inc(turned_stored, 16)

                def load_repeated():
                    sp.dma_start(repeated[:, :], rows(0, 0, DIST)).then_inc(repeated_loaded, 16)

                sp.wait_ge(turned_copied, G + 1)
                write(0)
                if positive(G):
                    sp.wait_ge(block_contracted, (G - 1) * BLOCKS + 1)
                write(1)
                sp.wait_ge(turned_stored, (G + 1) * 32)
                if not positive(G):
                    load_repeated()
                for t in range(FULL):
                    if t == FULL - 1 and positive(G):
                        sp.wait_ge(pairs_ready, G * BLOCKS)
                        load_repeated()
                    if t and positive(G):
                        sp.wait_ge(block_contracted, (G - 1) * BLOCKS + (t + 1))
                    sp.dma_start(pairs[:, t, :], rows(DIST * t, 1, DIST)).then_inc(moved_loaded[t], 16)
                if positive(G):
                    sp.wait_ge(last_low_ready, G)
                sp.dma_start(pairs[0:2 * FIELDS, FULL, :], rows(DIST * FULL, 0, 2)).then_inc(moved_loaded[FULL], 16)

            def batch_tile(bt):
                for g in range(GROUPS_OF_BT):
                    spread_group(bt * GROUPS_OF_BT + g, g % 2)

            batch_tile(0)
            with sp.Fori(1, BATCH_TILES) as bt:
                sp.wait_ge(rows_gathered, (bt + 1) * (16 * FIELDS))
                sp.dma_start(embedded[:, :, bass.ds(bt * WIDTH, WIDTH)],
                             gathered[:, :, :]).then_inc(embedded_ready, 16)
                batch_tile(bt)
            sp.wait_ge(y_ready, 2)
            sp.dma_start(out.rearrange("b o -> o b"), y_row[0:1, :]).then_inc(stored, 16)
            sp.wait_ge(stored, 16)

        @block.gpsimd
        def _(pool):
            nc.gpsimd.memset(identity[:, :], 1.0).then_inc(identity_blank, 1)
            pool.wait_ge(identity_blank, 1)
            nc.gpsimd.affine_select(out=identity[:, :], in_=identity[:, :], compare_op=ALU.is_equal,
                                    fill=0.0, base=0, pattern=[[-1, P]],
                                    channel_multiplier=1).then_inc(identity_ready, 1)

            def next_ids(bt):
                if positive(bt):
                    pool.wait_ge(ids_ready, bt)
                nc.gpsimd.tensor_copy(ids_now[:, :], ids_all[:, bass.ds(bt, 1), :].rearrange(
                    "p t f -> p (t f)")).then_inc(ids_ready, 1)
                pool.wait_ge(ids_ready, bt + 1)

            def gather(f, landing):
                pool.indirect_dma_start(landing[:, f, 0:WIDTH], None, tables[f][:, :],
                                        bass.IndirectOffsetOnAxis(ap=ids_now[:, f:f + 1], axis=0)
                                        ).then_inc(rows_gathered, 16)

            def fold_tile(group, j):
                before = group * FOLDS + j * 3
                pool.wait_ge(bank_scaled, group * (TILES * ACT_BANKS) + (j + 1) * ACT_BANKS)
                if positive(before):
                    pool.wait_ge(folded, before - (1 if j else 2))
                nc.gpsimd.tensor_tensor(fold1[:, :], scaled[:, j % 2, 0:1024], scaled[:, j % 2, 1024:2048],
                                        ALU.add).then_inc(folded, 1)
                pool.wait_ge(folded, before + 1)
                nc.gpsimd.tensor_tensor(fold2[:, :], fold1[:, 0:512], fold1[:, 512:1024],
                                        ALU.add).then_inc(folded, 1)
                pool.wait_ge(folded, before + 2)
                nc.gpsimd.tensor_tensor(fold3[:, j, :], fold2[:, 0:256], fold2[:, 256:512],
                                        ALU.add).then_inc(folded, 1)
                if j == TILES - 1:
                    pool.wait_ge(folded, before + 3)
                    if positive(group):
                        pool.wait_ge(total_ready, group)
                    nc.gpsimd.tensor_tensor(fold4[:, :].rearrange("p (j n) -> p j n", j=TILES),
                                            fold3[:, :, 0:MAPS], fold3[:, :, MAPS:2 * MAPS],
                                            ALU.add).then_inc(folded, 1)

            def batch_tile(bt, more1, more2):
                for n in range(GROUPS_OF_BT * TILES):
                    if more2 and n == FIRST_EARLY:
                        pool.wait_ge(rows_gathered, (bt + 2) * (16 * FIELDS))
                        pool.wait_ge(embedded_ready, (bt + 1) * 16)
                        next_ids(bt + 2)
                    fold_tile(bt * GROUPS_OF_BT + n // TILES, n % TILES)
                    if more1 and n < FIELDS - EARLY_FIELDS:
                        gather(EARLY_FIELDS + n, gathered)
                    if more2 and n >= FIRST_EARLY:
                        for f in range((n - FIRST_EARLY) * EARLY_FIELDS // EARLY_TILES,
                                       (n + 1 - FIRST_EARLY) * EARLY_FIELDS // EARLY_TILES):
                            gather(f, gathered)

            pool.wait_ge(ids_loaded, 16)
            next_ids(0)
            for f in range(FIELDS):
                gather(f, embedded)
            pool.wait_ge(rows_gathered, 16 * FIELDS)
            next_ids(1)
            for f in range(EARLY_FIELDS):
                gather(f, gathered)
            batch_tile(0, True, True)
            with pool.Fori(1, BATCH_TILES - 2) as bt:
                batch_tile(bt, True, True)
            batch_tile(BATCH_TILES - 2, True, False)
            batch_tile(BATCH_TILES - 1, False, False)

        @block.scalar
        def _(act):
            act.wait_ge(filter1_loaded, 16)
            nc.scalar.activation(filter1_high[:, :], filter1_full[:, :], ACT.Copy).then_inc(high_ready, 1)
            act.wait_ge(pair_sum_ready, 1)
            nc.scalar.activation(filter0_high[:, :, :], pair_sum[:, 0:FULL, :], ACT.Copy).then_inc(high_ready, 1)
            nc.scalar.activation(last_high.bitcast(fp32r), pair_sum[:, FULL, :], ACT.Copy).then_inc(high_ready, 1)

            def rows_of(G):
                return embedded[:, :, bass.ds(G * TILES, TILES)].rearrange("p f j -> p j f")

            def fields_can_be_taken(G):
                if positive(G // GROUPS_OF_BT):
                    act.wait_ge(embedded_ready, G // GROUPS_OF_BT * 16)
                if positive(G - 1):
                    act.wait_ge(unit_added, (G - 1) * (TILES * DVE_UNITS))
                    act.wait_ge(bank_scaled, (G - 1) * (TILES * ACT_BANKS))

            def take_fields(G, par):
                nc.scalar.activation(fields[:, par, :, :], rows_of(G), ACT.Copy).then_inc(fields_ready, 1)

            def early_can_be_taken(G):
                if positive(G // GROUPS_OF_BT):
                    act.wait_ge(embedded_ready, G // GROUPS_OF_BT * 16)
                if positive(G):
                    act.wait_ge(fields_turned, G)

            def take_early(G):
                nc.scalar.activation(early[:, :, :], embedded[:, :, bass.ds(G * TILES, TILES)],
                                     ACT.Copy).then_inc(early_ready, 1)

            def take_block_high(G, t):
                act.wait_ge(pairs_ready, G * BLOCKS + (t + 1))
                if positive(place_free_after(G, t)):
                    act.wait_ge(block_contracted, place_free_after(G, t))
                nc.scalar.activation(block_high[:, t % 2, :], pairs[:, t, :],
                                     ACT.Copy).then_inc(block_high_ready, 1)

            def take_last_high(G):
                act.wait_ge(pairs_ready, (G + 1) * BLOCKS)
                if positive(G):
                    act.wait_ge(block_contracted, G * BLOCKS)
                nc.scalar.activation(last_pairs[0:2 * FIELDS, :], pairs[0:2 * FIELDS, FULL, :],
                                     ACT.Copy).then_inc(last_high_ready, 1)

            def take_turned(G):
                act.wait_ge(fields_turned, G + 1)
                if positive(G):
                    act.wait_ge(turned_stored, G * 32)
                nc.scalar.activation(early_t[:, :], turned[0][:, 0:P], ACT.Copy).then_inc(turned_copied, 1)

            def take_maps(G, par):
                act.wait_ge(block_contracted, (G + 1) * BLOCKS)
                if positive(G - 1):
                    act.wait_ge(inner_ready, (G - 1) * SLOTS)
                nc.scalar.activation(maps_high[:, par, :], maps_sum[:, :],
                                     ACT.Relu).then_inc(maps_high_ready, 1)

            def group(G, par, more1, more2):
                for k in range(SLOTS):
                    j, b = k // FILLS, k % FILLS
                    if OWNER[b] == "V":
                        continue
                    if b == 0 and positive(G * TILES + (j - 1)):
                        act.wait_ge(folded, G * FOLDS + ((j - 2) * 3 + 1 if j >= 2 else (j + 2) * 3 + 1 - FOLDS))
                        act.wait_ge(unit_added, G * (TILES * DVE_UNITS) + ((j - 2) * DVE_UNITS + UNIT_H))
                    if more1 and k == FIELDS_AFTER:
                        fields_can_be_taken(G + 1)
                    if more2 and k == EARLY_AFTER:
                        early_can_be_taken(G + 2)
                    act.wait_ge(inner_ready, G * SLOTS + (k + 1))
                    for c in range(UNIT_H):
                        h = b * UNIT_H + c
                        if OWNER[b] == "X":
                            dst = extra[:, j % 2, c * MAPS:(c + 1) * MAPS]
                        else:
                            at = OWNER[:b].count("S") * COLS + c * MAPS
                            dst = scaled[:, j % 2, at:at + MAPS]
                        last = nc.scalar.activation(dst, inner[bank_of(k)][:, c * MAPS:(c + 1) * MAPS],
                                                    ACT.Copy, scale=fields[:, par, j, h:h + 1])
                    last.then_inc(bank_scaled, 1)
                    if more1 and k == FIELDS_AFTER:
                        take_fields(G + 1, 1 - par)
                    if more1 and k == LAST_HIGH_AFTER:
                        take_last_high(G + 1)
                    if more1 and k == MAPS_AFTER:
                        take_maps(G + 1, 1 - par)
                    if more2 and k == BLOCK_HIGH_AFTER[0]:
                        take_block_high(G + 2, 0)
                    if more1 and k in BLOCK_HIGH_AFTER[1:]:
                        take_block_high(G + 1, BLOCK_HIGH_AFTER.index(k))
                    if more2 and k == EARLY_AFTER:
                        take_early(G + 2)
                    if more2 and k == TURNED_AFTER:
                        take_turned(G + 2)

            act.wait_ge(rows_gathered, 16 * FIELDS)
            take_early(0)
            take_fields(0, 0)
            take_turned(0)
            early_can_be_taken(1)
            take_early(1)
            take_turned(1)
            for t in range(FULL):
                take_block_high(0, t)
            take_last_high(0)
            take_maps(0, 0)
            take_block_high(1, 0)
            group(0, 0, True, True)
            group(1, 1, True, True)
            with act.Fori(1, GROUPS // 2 - 1) as pair:
                group(pair * 2, 0, True, True)
                group(pair * 2 + 1, 1, True, True)
            group(GROUPS - 2, 0, True, False)
            group(GROUPS - 1, 1, False, False)

            act.wait_ge(top_loaded, 16 * 8)
            for n, (half, layer, o) in enumerate(mlp_steps):
                act.wait_ge(hidden_summed, n + 1)
                dst, bias = (hidden1, bias1) if layer == 1 else (hidden2, bias2)
                nc.scalar.activation(dst[:, o, half * 512:(half + 1) * 512], inner[n % RING][:, :],
                                     ACT.Relu, bias=bias[:, o:o + 1]).then_inc(hidden_ready, 1)
            for half in range(2):
                act.wait_ge(y_summed, half + 1)
                nc.scalar.activation(y_row[0:1, half * 512:(half + 1) * 512], turned[half][0:1, :],
                                     ACT.Copy).then_inc(y_ready, 1)

        @block.vector
        def _(dve):
            nc.vector.memset(pair_both[:, 0, 1, :], 0.0).then_inc(blanks_ready, 1)
            nc.vector.memset(pair_both[:, FULL, :, :], 0.0).then_inc(blanks_ready, 1)
            dve.wait_ge(identity_ready, 1)
            nc.vector.tensor_reduce(field_match[:, :], identity[:, :].rearrange("p (q f) -> p f q", f=FIELDS),
                                    AX.X, ALU.add).then_inc(match_ready, 1)
            dve.wait_ge(match_ready, 1)
            nc.vector.tensor_reduce(takes_high[:, :], field_match[:, 0:FIELDS // 2], AX.X,
                                    ALU.add).then_inc(last_filter_steps, 1)
            nc.vector.tensor_reduce(takes_low[:, :], field_match[:, FIELDS // 2:FIELDS], AX.X,
                                    ALU.add).then_inc(last_filter_steps, 1)
            nc.vector.memset(dense_in[:, :, :], 0.0).then_inc(blanks_ready, 1)
            nc.vector.memset(top1[:, 2, :], 0.0).then_inc(blanks_ready, 1)
            nc.vector.memset(last_pairs[2 * FIELDS:P, :].bitcast(fp32), 0.0).then_inc(last_filter_steps, 1)
            nc.vector.memset(pooled0_wide[:, :], 0.0).then_inc(pooled0_added, 1)
            dve.wait_ge(high_ready, 1)
            nc.vector.tensor_tensor(filter1_low[:, :], filter1_full[:, :],
                                    filter1_high[:, :].bitcast(fp32), ALU.subtract).then_inc(low_ready, 1)
            dve.wait_ge(low_ready, 1)
            nc.vector.memset(pooled1_wide[:, :], 0.0).then_inc(pooled1_added, 1)
            dve.wait_ge(filter0_loaded, 16 * PAIR_LOADS)
            nc.vector.tensor_tensor(pair_sum[:, :, :], pair_both[:, :, 0, :], pair_both[:, :, 1, :],
                                    ALU.add).then_inc(pair_sum_ready, 1)
            dve.wait_ge(pair_sum_ready, 1)
            dve.wait_ge(high_ready, 2)
            nc.vector.tensor_tensor(filter0_low[:, :, :], pair_sum[:, 0:FULL, :],
                                    filter0_high[:, :, :].bitcast(fp32), ALU.subtract).then_inc(low_ready, 1)
            dve.wait_ge(high_ready, 3)
            nc.vector.tensor_tensor(last_low[:, :], pair_sum[:, FULL, :], last_high,
                                    ALU.subtract).then_inc(last_filter_steps, 1)
            dve.wait_ge(last_filter_steps, 4)
            nc.vector.tensor_scalar(last_low[:, :], last_low[:, :], takes_low[:, 0:1], None,
                                    ALU.mult).then_inc(last_filter_steps, 1)
            dve.wait_ge(last_filter_steps, 5)
            nc.vector.scalar_tensor_tensor(out=last_filter[:, :], in0=last_high,
                                           scalar=takes_high[:, 0:1], in1=last_low[:, :],
                                           op0=ALU.mult, op1=ALU.add).then_inc(last_filter_steps, 1)

            def make_pairs(G, t):
                rows = slice(0, P if t < FULL else 2 * FIELDS)
                dve.wait_ge(repeated_loaded, (G + 1) * 16)
                dve.wait_ge(moved_loaded[t], (G + 1) * 16)
                nc.vector.tensor_tensor(pairs[rows, t, :], pairs[rows, t, :], repeated[rows, :],
                                        ALU.mult).then_inc(pairs_ready, 1)

            def take_block_low(G, t):
                dve.wait_ge(block_high_ready, G * FULL + (t + 1))
                if positive(place_free_after(G, t)):
                    dve.wait_ge(block_contracted, place_free_after(G, t))
                at = t % 2
                nc.vector.tensor_tensor(block_low[:, at, :], pairs[:, t, :], block_high[:, at, :].bitcast(fp32),
                                        ALU.subtract).then_inc(block_low_ready, 1)

            def take_last_low(G):
                dve.wait_ge(last_high_ready, G + 1)
                rows = slice(FIELDS, 2 * FIELDS)
                nc.vector.tensor_tensor(last_pairs[rows, :], pairs[rows, FULL, :],
                                        last_pairs[rows, :].bitcast(fp32), ALU.subtract).then_inc(last_low_ready, 1)

            def split_maps(G, par):
                dve.wait_ge(maps_high_ready, G + 1)
                nc.vector.scalar_tensor_tensor(out=maps_low[:, par, :], in0=maps_sum[:, :], scalar=0.0,
                                               in1=maps_high[:, par, :].bitcast(fp32), op0=ALU.max,
                                               op1=ALU.subtract).then_inc(maps_low_ready, 1)

            def pool_maps(G):
                dve.wait_ge(maps_high_ready, G + 1)
                dve.wait_ge(pooled0_added, G + 1)
                acc = pooled0_wide[:, bass.ds(G // GROUPS_OF_BT * COLS, COLS)]
                nc.vector.scalar_tensor_tensor(out=acc, in0=maps_sum[:, :], scalar=0.0, in1=acc,
                                               op0=ALU.max, op1=ALU.add).then_inc(pooled0_added, 1)

            def halve_lanes(G, par):
                dve.wait_ge(pooled1_added, G + 1)
                dve.wait_ge(unit_added, (G + 1) * (TILES * DVE_UNITS))
                nc.vector.tensor_tensor(lanes_half[:, :].rearrange("p (a n) -> p a n", a=2),
                                        lanes[:, par, 0:2, :], lanes[:, par, 2:4, :],
                                        ALU.add).then_inc(lanes_halved, 1)

            def sum_lanes(G):
                dve.wait_ge(lanes_halved, G + 1)
                nc.vector.tensor_tensor(lanes_sum[:, :], lanes_half[:, 0:COLS], lanes_half[:, COLS:2 * COLS],
                                        ALU.add).then_inc(lanes_summed, 1)

            def sum_total(G):
                dve.wait_ge(lanes_summed, G + 1)
                dve.wait_ge(folded, (G + 1) * FOLDS)
                nc.vector.tensor_tensor(total[:, :], lanes_sum[:, :], fold4[:, :],
                                        ALU.add).then_inc(total_ready, 1)

            def pool_total(G):
                dve.wait_ge(total_ready, G + 1)
                dve.wait_ge(pooled1_added, G + 1)
                acc = pooled1_wide[:, bass.ds(G // GROUPS_OF_BT * COLS, COLS)]
                nc.vector.scalar_tensor_tensor(out=acc, in0=total[:, :], scalar=0.0, in1=acc,
                                               op0=ALU.max, op1=ALU.add).then_inc(pooled1_added, 1)

            def fold_pooled(wide, narrow, first, end):
                v = wide[:, first * COLS:end * COLS].rearrange("p (t j n) -> p t n j", j=TILES, n=P)
                nc.vector.tensor_reduce(narrow[:, first * P:end * P].rearrange("p (t n) -> p t n", n=P), v,
                                        AX.X, ALU.add).then_inc(pooled_folded, 1)

            def copy_turned(half):
                for src, dst in ((0, pooled1_t), (1, dense_t)):
                    dve.wait_ge(top_turned, half * 2 + src + 1)
                    nc.vector.tensor_copy(dst[:, half * 512:(half + 1) * 512],
                                          turned[src][:, :]).then_inc(top_turned_copied, 1)

            def group(G, par, more1, more2):
                for k in range(SLOTS):
                    j, b = k // FILLS, k % FILLS
                    if OWNER[b] != "V":
                        continue
                    n_before = OWNER[:b].count("V") * UNIT_H
                    if n_before == 0:
                        dve.wait_ge(bank_scaled, G * (TILES * ACT_BANKS) + (j * ACT_BANKS + 1))
                        if positive(G - 1):
                            dve.wait_ge(lanes_halved, G - 1)
                    dve.wait_ge(inner_ready, G * SLOTS + (k + 1))
                    for c in range(UNIT_H):
                        h = b * UNIT_H + c
                        acc = lanes[:, par, c, j * MAPS:(j + 1) * MAPS]
                        before = extra[:, j % 2, c * MAPS:(c + 1) * MAPS] if n_before == 0 else acc
                        if n_before:
                            dve.wait_ge(unit_added, G * (TILES * DVE_UNITS)
                                        + (j * DVE_UNITS + n_before + c - UNIT_H + 1))
                        nc.vector.scalar_tensor_tensor(out=acc, in0=inner[bank_of(k)][:, c * MAPS:(c + 1) * MAPS],
                                                       scalar=fields[:, par, j, h:h + 1], in1=before,
                                                       op0=ALU.mult, op1=ALU.add).then_inc(unit_added, 1)
                    if not more1 and k in HALF_FOLD_AFTER:
                        n = HALF_FOLD_AFTER.index(k)
                        if n == 0:
                            dve.wait_ge(pooled0_added, GROUPS)
                        wide, narrow = ((pooled0_wide, pooled0), (pooled1_wide, pooled1))[n // 2]
                        fold_pooled(wide, narrow, n % 2 * 2, (n % 2 + 1) * 2)
                    if not more1 and k == HALF_COPY_AFTER:
                        copy_turned(0)
                    if positive(G) and k == LANES_AFTER:
                        halve_lanes(G - 1, 1 - par)
                    if positive(G) and k == LANES_SUM_AFTER:
                        sum_lanes(G - 1)
                    if positive(G) and k == TOTAL_AFTER:
                        sum_total(G - 1)
                    if positive(G) and k == POOL_TOTAL_AFTER:
                        pool_total(G - 1)
                    if k == POOL_MAPS_AFTER:
                        pool_maps(G)
                    if more1 and k in PAIRS_AFTER[1:]:
                        make_pairs(G + 1, PAIRS_AFTER.index(k))
                    if more2 and k == BLOCK_LOW_AFTER[0]:
                        take_block_low(G + 2, 0)
                    if more1 and k in BLOCK_LOW_AFTER[1:]:
                        take_block_low(G + 1, BLOCK_LOW_AFTER.index(k))
                    if more1 and k == LAST_LOW_AFTER:
                        take_last_low(G + 1)
                    if more1 and k == SPLIT_AFTER:
                        split_maps(G + 1, 1 - par)
                    if more2 and k == PAIRS_AFTER[0]:
                        make_pairs(G + 2, 0)

            make_pairs(0, 0)
            for t in range(FULL):
                make_pairs(0, t + 1)
                take_block_low(0, t)
            take_last_low(0)
            split_maps(0, 0)
            make_pairs(1, 0)
            take_block_low(1, 0)
            group(0, 0, True, True)
            group(1, 1, True, True)
            with dve.Fori(1, GROUPS // 2 - 1) as pair:
                group(pair * 2, 0, True, True)
                group(pair * 2 + 1, 1, True, True)

            half_tiles = BATCH_TILES // 2
            group(GROUPS - 2, 0, True, False)
            group(GROUPS - 1, 1, False, False)
            halve_lanes(GROUPS - 1, 1)
            dve.wait_ge(pooled0_added, GROUPS + 1)
            fold_pooled(pooled0_wide, pooled0, half_tiles, BATCH_TILES)
            sum_lanes(GROUPS - 1)
            fold_pooled(pooled1_wide, pooled1, half_tiles, BATCH_TILES - 1)
            sum_total(GROUPS - 1)
            pool_total(GROUPS - 1)
            dve.wait_ge(pooled1_added, GROUPS + 1)
            fold_pooled(pooled1_wide, pooled1, BATCH_TILES - 1, BATCH_TILES)
            copy_turned(1)

        @block.tensor
        def _(pe):
            def turn_fields(G):
                pe.wait_ge(early_ready, G + 1)
                if positive(G):
                    pe.wait_ge(turned_copied, G)
                nc.tensor.transpose(turned[0][:, 0:P], early[:, :, :].rearrange("p f j -> p (f j)"),
                                    identity[:, :]).then_inc(fields_turned, 1)

            def contract(G, t):
                if t == 0 and positive(G):
                    pe.wait_ge(maps_low_ready, G)
                    pe.wait_ge(pooled0_added, G + 1)
                pe.wait_ge(block_low_ready, G * FULL + (t + 1))
                high, low = block_high[:, t % 2, :], block_low[:, t % 2, :]
                nc.tensor.matmul(maps_sum[:, :], filter0_high[:, t, :], low, start=(t == 0), stop=False)
                nc.tensor.matmul(maps_sum[:, :], filter0_low[:, t, :], high, start=False, stop=False)
                last = nc.tensor.matmul(maps_sum[:, :], filter0_high[:, t, :], high, start=False, stop=False)
                last.then_inc(block_contracted, 1)

            def contract_last(G):
                pe.wait_ge(last_low_ready, G + 1)
                nc.tensor.matmul(maps_sum[:, :], last_filter[:, :], last_pairs[:, :], start=False,
                                 stop=True).then_inc(block_contracted, 1)

            def turn_half(half):
                pe.wait_ge(pooled_folded, 4 + 3 * half)
                if half == 0:
                    pe.wait_ge(top_loaded, 16 * 8)
                    pe.wait_ge(pooled0_added, GROUPS + 1)
                else:
                    pe.wait_ge(top_turned_copied, 2)
                for src in range(2):
                    for j in range(TILES):
                        bt = half * TILES + j
                        a = pooled1[:, bt * P:(bt + 1) * P] if src == 0 else dense_in[:, bt, :]
                        last = nc.tensor.transpose(turned[src][:, j * P:(j + 1) * P], a, identity[:, :])
                    last.then_inc(top_turned, 1)

            def group(G, par, more1, more2):
                pe.wait_ge(maps_low_ready, G + 1)
                for k in range(SLOTS):
                    j, b = k // FILLS, k % FILLS
                    if more1 and k in CONTRACT_AT[:FULL]:
                        contract(G + 1, CONTRACT_AT.index(k))
                    if more1 and k == CONTRACT_AT[FULL]:
                        contract_last(G + 1)
                    if not more1 and k == HALF_TURN_AT:
                        turn_half(0)
                    if more2 and k == TURN_AT:
                        turn_fields(G + 2)
                    if OWNER[b] == "V":
                        used = slots_of("V", k) - V_RING + 1
                        if positive(G * SLOTS + used):
                            pe.wait_ge(unit_added, (G * (TILES * DVE_UNITS) + used * UNIT_H))
                    else:
                        used = slots_of("SX", k) - S_RING + 1
                        if positive(G * SLOTS + used):
                            pe.wait_ge(bank_scaled, G * (TILES * ACT_BANKS) + used)
                    high = maps_high[:, par, j * P:(j + 1) * P]
                    low = maps_low[:, par, j * P:(j + 1) * P]
                    cols = slice(b * COLS, (b + 1) * COLS)
                    y = inner[bank_of(k)]
                    nc.tensor.matmul(y[:, :], low, filter1_high[:, cols], start=True, stop=False)
                    nc.tensor.matmul(y[:, :], high, filter1_low[:, cols], start=False, stop=False)
                    nc.tensor.matmul(y[:, :], high, filter1_high[:, cols], start=False,
                                     stop=True).then_inc(inner_ready, 1)

            pe.wait_ge(identity_ready, 1)
            turn_fields(0)
            turn_fields(1)
            pe.wait_ge(low_ready, 2)
            for t in range(FULL):
                contract(0, t)
            pe.wait_ge(last_filter_steps, 6)
            contract_last(0)
            group(0, 0, True, True)
            group(1, 1, True, True)
            with pe.Fori(1, GROUPS // 2 - 1) as pair:
                group(pair * 2, 0, True, True)
                group(pair * 2 + 1, 1, True, True)
            group(GROUPS - 2, 0, True, False)
            group(GROUPS - 1, 1, False, False)

            pe.wait_ge(unit_added, GROUPS * TILES * DVE_UNITS)
            pe.wait_ge(bank_scaled, GROUPS * TILES * ACT_BANKS)
            for n, (half, layer, o) in enumerate(mlp_steps):
                cols = slice(half * 512, (half + 1) * 512)
                if n >= RING:
                    pe.wait_ge(hidden_ready, n - RING + 1)
                if layer == 1:
                    if half == 1 and o == 0:
                        turn_half(1)
                    pe.wait_ge(top_turned_copied, 2 * (half + 1))
                    terms = [(top1[:, k, o * P:(o + 1) * P], rhs[:, cols])
                             for k, rhs in enumerate((pooled0, pooled1_t, dense_t))]
                else:
                    pe.wait_ge(hidden_ready, steps_through(half, 1))
                    terms = [(top2[:, k, o * P:(o + 1) * P], hidden1[:, k, cols]) for k in range(HID1 // P)]
                for k, (w, x) in enumerate(terms):
                    last = nc.tensor.matmul(inner[n % RING][:, :], w, x, start=(k == 0),
                                            stop=(k == len(terms) - 1))
                last.then_inc(hidden_summed, 1)
            for half in range(2):
                pe.wait_ge(hidden_ready, steps_through(half, 2))
                for k in range(HID2 // P):
                    last = nc.tensor.matmul(turned[half][0:1, :], top3[:, k:k + 1],
                                            hidden2[:, k, half * 512:(half + 1) * 512],
                                            start=(k == 0), stop=(k == HID2 // P - 1))
                last.then_inc(y_summed, 1)


_INS = (["dense_ctx", "ids"] + [f"tbl_{f}" for f in range(FIELDS)]
        + ["W_top1", "b_top1", "W_top2", "b_top2", "W_top3", "L0_rec_filter_0", "L0_rec_filter_1"])


def kernel(**inputs):
    import numpy as _np
    import concourse.bacc as _bacc
    from concourse import mybir as _mybir
    from concourse.bass_utils import run_bass_kernel_spmd as _run

    nc = _bacc.Bacc("TRN2", target_bir_lowering=False, num_devices=1)
    arrays, ap = {}, {}
    for name in _INS:
        a = _np.ascontiguousarray(inputs[name])
        arrays[f"in_{name}"] = a
        ap[name] = nc.dram_tensor(f"in_{name}", a.shape, _mybir.dt.from_np(a.dtype), kind="ExternalInput").ap()
    out = nc.dram_tensor("out_y", (BATCH, 1), _mybir.dt.float32, kind="ExternalOutput").ap()
    dlrm_tower(nc, ap["dense_ctx"], ap["ids"], [ap[f"tbl_{f}"] for f in range(FIELDS)], ap["W_top1"],
               ap["b_top1"], ap["W_top2"], ap["b_top2"], ap["W_top3"], ap["L0_rec_filter_0"],
               ap["L0_rec_filter_1"], out)
    r = _run(nc, [arrays], core_ids=[0])
    return r.results[0]["out_y"]
```
